# Optimizing a Trainium2 kernel written in Bass

```python
import numpy as np
import jax
import jax.numpy as jnp

def _softmax(x, axis=-1):
    return jax.nn.softmax(x, axis=axis)

def _gelu(x):
    return jax.nn.gelu(x, approximate=True)

def _silu(x):
    return jax.nn.silu(x)

def _sigmoid(x):
    return jax.nn.sigmoid(x)

def _layernorm(x, axis=-1, eps=1e-05):
    m = jnp.mean(x, axis=axis, keepdims=True)
    v = jnp.var(x, axis=axis, keepdims=True)
    return (x - m) / jnp.sqrt(v + eps)

def _scatter_add(tgt, idx, src, axis=0):
    return tgt.at[idx].add(src)

def _segment_sum(src, seg, n):
    return jax.ops.segment_sum(src, seg, n)
kernel_name = 'mk_seq_preln_d1_jaxref_r4_0c29ff'

def setup_inputs(seed: int=0):
    np.random.seed(seed)
    _w = jnp.asarray

    def _L0_attn_setup():
        import jax, jax.numpy as jnp
        import numpy as np
        B, S, D = (2, 512, 512)
        H, HD = (16, 128)
        RD = 64
        ND = HD - RD
        KVR, QR = (128, 256)
        BASE = 10000.0
        NEG = -1e+30

        def _apply_rope(t):
            half = RD // 2
            seq = t.shape[2]
            inv_freq = 1.0 / BASE ** (jnp.arange(half, dtype=jnp.float32) / half)
            ang = jnp.arange(seq, dtype=jnp.float32)[:, None] * inv_freq
            cos, sin = (jnp.cos(ang), jnp.sin(ang))
            t1, t2 = (t[..., :half], t[..., half:])
            return jnp.concatenate([t1 * cos - t2 * sin, t1 * sin + t2 * cos], axis=-1)
        key = jax.random.key(seed)
        ks = jax.random.split(key, 9)

        def w(k, shape):
            return jax.random.normal(k, shape, jnp.float32) * shape[0] ** (-0.5)
        return {'x': jax.random.normal(ks[0], (B, S, D), jnp.float32), 'Wq_down': w(ks[1], (D, QR)), 'Wq_up': w(ks[2], (QR, H * ND)), 'Wq_rope': w(ks[3], (QR, H * RD)), 'Wkv_down': w(ks[4], (D, KVR)), 'Wk_up': w(ks[5], (KVR, H * ND)), 'Wk_rope': w(ks[6], (D, H * RD)), 'Wv_up': w(ks[7], (KVR, H * HD)), 'Wo': w(ks[8], (H * HD, D))}
    _L0_attn_in = _L0_attn_setup()

    def _L0_ffn_setup():
        import jax, jax.numpy as jnp
        import numpy as np
        D_MODEL = 512
        D_EXPERT = 2048
        EPS = 1e-08

        def ternary_quant(w):
            scale = jnp.mean(jnp.abs(w)) + EPS
            q = jnp.clip(jnp.round(w / scale), -1.0, 1.0) * scale
            return w + jax.lax.stop_gradient(q - w)
        key = jax.random.key(seed)
        k_x, k_up, k_gate, k_down = jax.random.split(key, 4)
        std_in = 1.0 / np.sqrt(D_MODEL)
        std_exp = 1.0 / np.sqrt(D_EXPERT)
        return {'x': jax.random.normal(k_x, (4, 512, D_MODEL), dtype=jnp.float32), 'W_up': jax.random.normal(k_up, (D_EXPERT, D_MODEL), dtype=jnp.float32) * std_in, 'W_gate': jax.random.normal(k_gate, (D_EXPERT, D_MODEL), dtype=jnp.float32) * std_in, 'W_down': jax.random.normal(k_down, (D_MODEL, D_EXPERT), dtype=jnp.float32) * std_exp}
    _L0_ffn_in = _L0_ffn_setup()
    _d = {'L0_attn_x': _L0_attn_in['x'], 'L0_attn_Wq_down': _L0_attn_in['Wq_down'], 'L0_attn_Wq_up': _L0_attn_in['Wq_up'], 'L0_attn_Wq_rope': _L0_attn_in['Wq_rope'], 'L0_attn_Wkv_down': _L0_attn_in['Wkv_down'], 'L0_attn_Wk_up': _L0_attn_in['Wk_up'], 'L0_attn_Wk_rope': _L0_attn_in['Wk_rope'], 'L0_attn_Wv_up': _L0_attn_in['Wv_up'], 'L0_attn_Wo': _L0_attn_in['Wo'], 'L0_ffn_W_up': _L0_ffn_in['W_up'], 'L0_ffn_W_gate': _L0_ffn_in['W_gate'], 'L0_ffn_W_down': _L0_ffn_in['W_down']}
    _x0 = _d['L0_attn_x']
    _d['L0_attn_x'] = jax.random.normal(jax.random.fold_in(jax.random.key(seed), 1), (1, 2048, 512), dtype=_x0.dtype)
    del _x0
    return _d

def reference(L0_attn_x, L0_attn_Wq_down, L0_attn_Wq_up, L0_attn_Wq_rope, L0_attn_Wkv_down, L0_attn_Wk_up, L0_attn_Wk_rope, L0_attn_Wv_up, L0_attn_Wo, L0_ffn_W_up, L0_ffn_W_gate, L0_ffn_W_down):

    def _L0_attn_ref(x, Wq_down, Wq_up, Wq_rope, Wkv_down, Wk_up, Wk_rope, Wv_up, Wo):
        import jax, jax.numpy as jnp
        import numpy as np
        B, S, D = (2, 512, 512)
        H, HD = (16, 128)
        RD = 64
        ND = HD - RD
        KVR, QR = (128, 256)
        BASE = 10000.0
        NEG = -1e+30

        def _apply_rope(t):
            half = RD // 2
            seq = t.shape[2]
            inv_freq = 1.0 / BASE ** (jnp.arange(half, dtype=jnp.float32) / half)
            ang = jnp.arange(seq, dtype=jnp.float32)[:, None] * inv_freq
            cos, sin = (jnp.cos(ang), jnp.sin(ang))
            t1, t2 = (t[..., :half], t[..., half:])
            return jnp.concatenate([t1 * cos - t2 * sin, t1 * sin + t2 * cos], axis=-1)
        b, s, _ = x.shape
        q_lat = x @ Wq_down
        q_nope = (q_lat @ Wq_up).reshape(b, s, H, ND).transpose(0, 2, 1, 3)
        q_pe = (q_lat @ Wq_rope).reshape(b, s, H, RD).transpose(0, 2, 1, 3)
        kv_lat = x @ Wkv_down
        k_nope = (kv_lat @ Wk_up).reshape(b, s, H, ND).transpose(0, 2, 1, 3)
        k_pe = (x @ Wk_rope).reshape(b, s, H, RD).transpose(0, 2, 1, 3)
        v = (kv_lat @ Wv_up).reshape(b, s, H, HD).transpose(0, 2, 1, 3)
        q_pe = _apply_rope(q_pe)
        k_pe = _apply_rope(k_pe)
        q = jnp.concatenate([q_nope, q_pe], axis=-1)
        k = jnp.concatenate([k_nope, k_pe], axis=-1)
        scale = HD ** (-0.5)
        scores = jnp.einsum('bhqd,bhkd->bhqk', q, k) * scale
        causal = jnp.tril(jnp.ones((s, s), dtype=bool))
        scores = jnp.where(causal, scores, NEG)
        attn = jax.nn.softmax(scores, axis=-1)
        out = jnp.einsum('bhqk,bhkd->bhqd', attn, v)
        out = out.transpose(0, 2, 1, 3).reshape(b, s, H * HD)
        return out @ Wo

    def _L0_ffn_ref(x, W_up, W_gate, W_down):
        import jax, jax.numpy as jnp
        import numpy as np
        D_MODEL = 512
        D_EXPERT = 2048
        EPS = 1e-08

        def ternary_quant(w):
            scale = jnp.mean(jnp.abs(w)) + EPS
            q = jnp.clip(jnp.round(w / scale), -1.0, 1.0) * scale
            return w + jax.lax.stop_gradient(q - w)
        wu = ternary_quant(W_up)
        wg = ternary_quant(W_gate)
        wd = ternary_quant(W_down)
        up = jnp.einsum('bsd,ed->bse', x, wu)
        gate = jnp.einsum('bsd,ed->bse', x, wg)
        hidden = jax.nn.silu(up) * gate
        return jnp.einsum('bse,de->bsd', hidden, wd)
    x = L0_attn_x
    x = x + _L0_attn_ref(_layernorm(x, axis=-1), L0_attn_Wq_down, L0_attn_Wq_up, L0_attn_Wq_rope, L0_attn_Wkv_down, L0_attn_Wk_up, L0_attn_Wk_rope, L0_attn_Wv_up, L0_attn_Wo)
    x = x + _L0_ffn_ref(_layernorm(x, axis=-1), L0_ffn_W_up, L0_ffn_W_gate, L0_ffn_W_down)
    return x

_drawn_inputs = setup_inputs


def setup_inputs(seed=0):
    import zlib

    import numpy as np

    out = dict(_drawn_inputs(seed))
    spreads = {}
    factors = {}
    for name, (base, spread) in spreads.items():
        noise = np.random.default_rng([zlib.crc32(name.encode()), seed]).standard_normal(out[name].shape)
        drawn = base * np.exp(spread * noise) if base else spread * noise
        out[name] = jnp.asarray(drawn.astype(out[name].dtype))
    for name, factor in factors.items():
        out[name] = (out[name] * factor).astype(out[name].dtype)
    return out
```

```python
from contextlib import ExitStack

import numpy as np

import concourse.bass as bass
from concourse import mybir

ALU = mybir.AluOpType
ACT = mybir.ActivationFunctionType
AX_X = mybir.AxisListType.X
F32 = mybir.dt.float32
F32R = mybir.dt.float32r
BF16 = mybir.dt.bfloat16

P = 128
LN_EPS = 1e-5
QUANT_EPS = 1e-8
NEG = -1e30
ROPE_BASE = 10000.0

T, D = 2048, 512
H, HD, RD = 16, 128, 64
HALF = RD // 2
ND = HD - RD
QR, KVR = 256, 128
E = 2048
KD = D // P
KQ = QR // P
NT = T // P
CH = 512
NC = T // CH
PAIRS = H // 2
SCALE = float(HD) ** -0.5


def parts(hi, lo):
    return ((hi, hi), (hi, lo), (lo, hi))


def latents(nc, hbm, keep, xT, qlatT, kvT):
    ident, kv = keep["ident"], keep["kv"]
    NL = KQ + 1
    LAT0 = 2
    with ExitStack() as ctx:
        def sb(name, shape, dt=F32):
            return ctx.enter_context(nc.sbuf_tensor(name, shape, dt))

        def sem(name):
            return ctx.enter_context(nc.semaphore(name))

        x = sb("x", [P, NT, D])
        w_raw = sb("wlat_raw", [P, KD, QR + KVR])
        w = [sb(f"wlat_{n}", [P, KD, QR + KVR], F32R) for n in ("hi", "lo")]
        bn = sb("bn", [P, 2, 6])
        mv = sb("mv", [P, NT, 2])
        std = sb("std", [P, NT])
        rstd = sb("rstd", [P, NT])
        xn = sb("xn", [P, 2, D])
        ps = ctx.enter_context(nc.psum_tensor("ps_lat", [P, 8, CH], F32))

        ident_loaded = sem("ident_loaded")
        x_loaded = [sem(f"x_loaded{i}") for i in range(4)]
        wlat_loaded = sem("wlat_loaded")
        stats_done = sem("stats_done")
        var_ready = sem("var_ready")
        std_ready = sem("std_ready")
        rstd_done = sem("rstd_done")
        xn_ready = sem("xn_ready")
        xt_ready = sem("xt_ready")
        xt_hi_ready = sem("xt_hi_ready")
        xt_lo_ready = sem("xt_lo_ready")
        wlat_hi_ready = sem("wlat_hi_ready")
        wlat_lo_ready = sem("wlat_lo_ready")
        lat_ready = sem("lat_ready")
        lat_hi_ready = sem("lat_hi_ready")
        lat_lo_ready = sem("lat_lo_ready")
        kv_hi_turned = sem("kv_hi_turned")
        kv_lo_turned = sem("kv_lo_turned")

        def lat(dst, m, c):
            cols = bass.ds(c * CH, CH)
            return qlatT[dst][:, m, cols] if m < KQ else kvT[dst][:, cols]

        block = ctx.enter_context(nc.Block())

        @block.sync
        def _(sp):
            sp.dma_start(ident[:], hbm["ident"]).then_inc(ident_loaded, 16)
            for q in range(4):
                sp.dma_start(x[:, 4 * q:4 * q + 4, :],
                             hbm["x"].rearrange("(t p) d -> p t d", p=P)[:, 4 * q:4 * q + 4, :]
                             ).then_inc(x_loaded[q], 16)
            sp.dma_start(w_raw[:, :, 0:QR],
                         hbm["Wq_down"].rearrange("(k p) n -> p k n", p=P)).then_inc(wlat_loaded, 16)
            sp.dma_start(w_raw[:, :, QR:QR + KVR],
                         hbm["Wkv_down"].rearrange("(k p) n -> p k n", p=P)).then_inc(wlat_loaded, 16)

        @block.vector
        def _(dve):
            for t in range(NT):
                if t % 4 == 0:
                    dve.wait_ge(x_loaded[t // 4], 16)
                nc.vector.bn_stats(bn[:, t % 2, :], x[:, t, :]).then_inc(stats_done, 1)
                dve.wait_ge(stats_done, 2 * t + 1)
                nc.vector.bn_aggr(mv[:, t, :], bn[:, t % 2, :]).then_inc(stats_done, 1)
            dve.wait_ge(stats_done, 2 * NT)
            nc.vector.tensor_scalar(std[:, :], mv[:, :, 1], LN_EPS, None, ALU.add).then_inc(var_ready, 1)
            dve.wait_ge(std_ready, 1)
            nc.vector.reciprocal(rstd[:, :], std[:, :]).then_inc(rstd_done, 1)
            dve.wait_ge(rstd_done, 1)
            with dve.Fori(0, NT // 2) as i:
                for j in range(2):
                    t = 2 * i + j
                    nc.vector.tensor_scalar(xn[:, j, :], x[:, bass.ds(t, 1), :],
                                            mv[:, bass.ds(t, 1), 0], rstd[:, bass.ds(t, 1)],
                                            ALU.subtract, ALU.mult).then_inc(xn_ready, 1)
                for j in range(2):
                    cols = bass.ds((2 * i + j) * P, P)
                    dve.wait_ge(xt_hi_ready, j + 1)
                    nc.vector.tensor_tensor(xT[1][:, :, cols],
                                            ps[:, j, :].rearrange("p (k n) -> p k n", k=KD),
                                            xT[0][:, :, cols].bitcast(F32),
                                            ALU.subtract).then_inc(xt_lo_ready, 1)
                dve.sem_inc(xt_hi_ready, -2)
            dve.wait_ge(wlat_hi_ready, 1)
            nc.vector.tensor_tensor(w[1][:], w_raw[:], w[0][:].bitcast(F32),
                                    ALU.subtract).then_inc(wlat_lo_ready, 1)
            with dve.Fori(0, NC) as c:
                for m in range(NL):
                    dve.wait_ge(lat_hi_ready, m + 1)
                    nc.vector.tensor_tensor(lat(1, m, c), ps[:, LAT0 + m, :], lat(0, m, c).bitcast(F32),
                                            ALU.subtract).then_inc(lat_lo_ready, 1)
                dve.sem_inc(lat_hi_ready, -NL)
            for b in range(NT // 4):
                dve.wait_ge(kv_lo_turned, b + 1)
                nc.vector.tensor_copy(kv[1][:, 4 * b:4 * b + 4, :],
                                      ps[:, 4 + b, :].rearrange("p (t n) -> p t n", t=4))

        @block.scalar
        def _(act):
            act.wait_ge(var_ready, 1)
            nc.scalar.activation(std[:, :], std[:, :], ACT.Sqrt).then_inc(std_ready, 1)
            act.wait_ge(wlat_loaded, 32)
            nc.scalar.copy(w[0][:], w_raw[:]).then_inc(wlat_hi_ready, 1)
            with act.Fori(0, NT // 2) as i:
                for j in range(2):
                    act.wait_ge(xt_ready, j + 1)
                    nc.scalar.copy(xT[0][:, :, bass.ds((2 * i + j) * P, P)],
                                   ps[:, j, :].rearrange("p (k n) -> p k n", k=KD)).then_inc(xt_hi_ready, 1)
                act.sem_inc(xt_ready, -2)
            with act.Fori(0, NC) as c:
                for m in range(NL):
                    act.wait_ge(lat_ready, m + 1)
                    nc.scalar.copy(lat(0, m, c), ps[:, LAT0 + m, :]).then_inc(lat_hi_ready, 1)
                act.sem_inc(lat_ready, -NL)
            for b in range(NT // 4):
                act.wait_ge(kv_hi_turned, b + 1)
                nc.scalar.copy(kv[0][:, 4 * b:4 * b + 4, :],
                               ps[:, b, :].rearrange("p (t n) -> p t n", t=4))

        @block.tensor
        def _(pe):
            pe.wait_ge(ident_loaded, 16)
            pe.sem_inc(xt_lo_ready, 2)
            with pe.Fori(0, NT // 2) as i:
                for j in range(2):
                    pe.wait_ge(xn_ready, j + 1)
                    pe.wait_ge(xt_lo_ready, j + 1)
                    for k in range(KD):
                        last = nc.tensor.transpose(ps[:, j, k * P:(k + 1) * P],
                                                   xn[:, j, k * P:(k + 1) * P], ident[:, :])
                    last.then_inc(xt_ready, 1)
                pe.sem_inc(xn_ready, -2)
                pe.sem_inc(xt_lo_ready, -2)
            pe.wait_ge(xt_lo_ready, 2)
            pe.wait_ge(wlat_lo_ready, 1)
            pe.sem_inc(lat_lo_ready, NL)
            with pe.Fori(0, NC) as c:
                for m in range(NL):
                    pe.wait_ge(lat_lo_ready, m + 1)
                    n = 0
                    for k in range(KD):
                        for a, b in parts(0, 1):
                            last = nc.tensor.matmul(ps[:, LAT0 + m, :], w[a][:, k, m * P:(m + 1) * P],
                                                    xT[b][:, k, bass.ds(c * CH, CH)],
                                                    start=(n == 0), stop=(n == 3 * KD - 1))
                            n += 1
                    last.then_inc(lat_ready, 1)
                pe.sem_inc(lat_lo_ready, -NL)
            pe.wait_ge(lat_lo_ready, NL)
            for b in range(NT // 4):
                for part, done in ((0, kv_hi_turned), (1, kv_lo_turned)):
                    for q in range(4):
                        t = 4 * b + q
                        last = nc.tensor.transpose(ps[:, 4 * part + b, q * P:(q + 1) * P],
                                                   kvT[part][:, t * P:(t + 1) * P].bitcast(F32), ident[:, :])
                    last.then_inc(done, 1)


def heads_inputs(nc, hbm, keep, xT, qlatT, kvT):
    ident = keep["ident"]
    ROT_Q, ROT_K, PLAIN_Q, PLAIN_K = 0, KQ, KQ + KD, 2 * KQ + KD
    NSL = 2 * KQ + KD + 1
    Q, K = 0, 1
    ROT = ((K, ROT_K, xT, KD), (Q, ROT_Q, qlatT, KQ))
    PLAIN = ((Q, PLAIN_Q, qlatT, KQ), (K, PLAIN_K, [z[:].rearrange("p (k n) -> p k n", k=1) for z in kvT], 1))
    PLAIN0, WV_BANK, WVO0 = 2, 4, 5
    with ExitStack() as ctx:
        def sb(name, shape, dt=F32):
            return ctx.enter_context(nc.sbuf_tensor(name, shape, dt))

        def sem(name):
            return ctx.enter_context(nc.semaphore(name))

        cos, sin = sb("cos", [P, T]), sb("sin", [P, T])
        w_raw = sb("w_raw", [P, NSL, P])
        w = [[sb(f"w_{n}{j}", [P, NSL, P], F32R) for n in ("hi", "lo")] for j in range(2)]
        wv_raw = sb("wv_raw", [P, 2, P])
        wvT = [sb(f"wvT_{n}", [P, 2, P], F32R) for n in ("hi", "lo")]
        wo_raw = sb("wo_raw", [P, 2, D])
        wo = [sb(f"wo_{n}", [P, 2, D], F32R) for n in ("hi", "lo")]
        wvo_out = sb("wvo_out", [P, 2, D])
        by_cos = sb("by_cos", [P, 2, CH])
        by_sin = sb("by_sin", [P, 2, CH])
        rot_out = sb("rot_out", [P, 2, CH])
        plain_out = sb("plain_out", [P, 2, CH])
        ps = ctx.enter_context(nc.psum_tensor("ps_proj", [P, 8, CH], F32))

        tables_loaded = sem("tables_loaded")
        w_loaded = sem("w_loaded")
        w_hi_ready = sem("w_hi_ready")
        w_lo_ready = sem("w_lo_ready")
        wv_turned = sem("wv_turned")
        wv_hi_ready = sem("wv_hi_ready")
        wv_lo_ready = sem("wv_lo_ready")
        wvo_ready = sem("wvo_ready")
        wvo_copied = sem("wvo_copied")
        wvo_stored = sem("wvo_stored")
        rot_ready = sem("rot_ready")
        rot_bank_free = sem("rot_bank_free")
        multiplied = sem("multiplied")
        rot_done = sem("rot_done")
        rot_stored = [sem(f"rot_stored{i}") for i in range(2)]
        plain_ready = sem("plain_ready")
        plain_bank_free = sem("plain_bank_free")
        plain_done = sem("plain_done")
        plain_stored = [sem(f"plain_stored{i}") for i in range(2)]

        NW = 6
        PER_PAIR = 2 * NC

        def load_weights(sp, pair):
            cols, heads = bass.ds(pair * P, P), bass.ds(pair * 2, 2)
            for name, s0, k in (("Wq_rope", ROT_Q, KQ), ("Wk_rope", ROT_K, KD),
                                ("Wq_up", PLAIN_Q, KQ), ("Wk_up", PLAIN_K, 1)):
                sp.dma_start(w_raw[:, s0:s0 + k, :],
                             hbm[name].rearrange("(k p) n -> p k n", p=P)[:, :, cols]).then_inc(w_loaded, 16)
            sp.dma_start(wv_raw[:], hbm["Wv_up"].rearrange("p (h n) -> p h n", n=P)[:, heads, :]
                         ).then_inc(w_loaded, 16)
            sp.dma_start(wo_raw[:], hbm["Wo"].rearrange("(h p) n -> p h n", p=P)[:, heads, :]
                         ).then_inc(w_loaded, 16)

        def rotary_views(j, part, f):
            raw = w_raw[:, 0:PLAIN_Q, :].rearrange("p k (h f r) -> p k f h r", h=2, f=2)[:, :, f]
            put = w[j][part][:, 0:PLAIN_Q, :].rearrange("p k (f h r) -> p k f h r", h=2, f=2)[:, :, f]
            return put, raw

        def split_hi(j):
            for f in range(2):
                put, raw = rotary_views(j, 0, f)
                nc.scalar.copy(put, raw)
            nc.scalar.copy(wo[0][:], wo_raw[:])
            nc.scalar.copy(w[j][0][:, PLAIN_Q:NSL, :], w_raw[:, PLAIN_Q:NSL, :]).then_inc(w_hi_ready, 1)

        def split_lo(j):
            for f in range(2):
                put, raw = rotary_views(j, 1, f)
                nc.gpsimd.tensor_tensor(put, raw, rotary_views(j, 0, f)[0].bitcast(F32), ALU.subtract)
            nc.gpsimd.tensor_tensor(wo[1][:], wo_raw[:], wo[0][:].bitcast(F32), ALU.subtract)
            nc.gpsimd.tensor_tensor(w[j][1][:, PLAIN_Q:NSL, :], w_raw[:, PLAIN_Q:NSL, :],
                                    w[j][0][:, PLAIN_Q:NSL, :].bitcast(F32),
                                    ALU.subtract).then_inc(w_lo_ready, 1)

        block = ctx.enter_context(nc.Block())

        @block.sync
        def _(sp):
            load_weights(sp, 0)
            sp.dma_start(cos[:], hbm["cos"]).then_inc(tables_loaded, 16)
            sp.dma_start(sin[:], hbm["sin"]).then_inc(tables_loaded, 16)
            with sp.Fori(0, PAIRS // 2) as i:
                for j in range(2):
                    pair = 2 * i + j
                    following = sp.snap((pair + 1) % PAIRS)
                    for c in range(NC):
                        toks = slice(c * CH, (c + 1) * CH)
                        for g in range(2):
                            n = PER_PAIR * j + 2 * c + g + 1
                            sp.wait_ge(plain_done, n)
                            sp.sem_inc(plain_bank_free, 1)
                            sp.dma_start(hbm["plainT"][PLAIN[g][0], bass.ds(pair, 1), :, toks],
                                         plain_out[:, g, :]).then_inc(plain_stored[g], 16)
                            sp.wait_ge(rot_done, n)
                            sp.sem_inc(rot_bank_free, 1)
                            sp.dma_start(hbm["rotT"][ROT[g][0], bass.ds(pair, 1), :, toks],
                                         rot_out[:, g, :]).then_inc(rot_stored[g], 16)
                        if c == 0:
                            load_weights(sp, following)
                    sp.wait_ge(wvo_copied, j + 1)
                    sp.dma_start(hbm["wvo"].rearrange("(h p) n -> p h n", p=P)[:, bass.ds(2 * following, 2), :],
                                 wvo_out[:]).then_inc(wvo_stored, 16)
                sp.sem_inc(plain_done, -2 * PER_PAIR)
                sp.sem_inc(rot_done, -2 * PER_PAIR)
                sp.sem_inc(wvo_copied, -2)

        @block.scalar
        def _(act):
            for s in (*plain_stored, wvo_stored):
                act.sem_inc(s, 16)
            act.wait_ge(w_loaded, 16 * NW)
            act.sem_inc(w_loaded, -16 * NW)
            split_hi(0)
            with act.Fori(0, PAIRS // 2) as i:
                for j in range(2):
                    for c in range(NC):
                        for g in range(2):
                            act.wait_ge(plain_ready, PER_PAIR * j + 2 * c + g + 1)
                            act.wait_ge(plain_stored[g], 16)
                            act.sem_inc(plain_stored[g], -16)
                            nc.scalar.copy(plain_out[:, g, :], ps[:, PLAIN0 + g, :]).then_inc(plain_done, 1)
                        if c == 1:
                            act.wait_ge(w_loaded, 16 * NW * (j + 1))
                            split_hi(1 - j)
                        if c == 2:
                            act.wait_ge(wv_turned, j + 1)
                            nc.scalar.copy(wvT[0][:], ps[:, WV_BANK, 0:2 * P].rearrange("p (h n) -> p h n", h=2)
                                           ).then_inc(wv_hi_ready, 1)
                    act.wait_ge(wvo_ready, j + 1)
                    act.wait_ge(wvo_stored, 16)
                    act.sem_inc(wvo_stored, -16)
                    nc.scalar.copy(wvo_out[:], ps[:, WVO0:WVO0 + 2, :]).then_inc(wvo_copied, 1)
                act.sem_inc(plain_ready, -2 * PER_PAIR)
                act.sem_inc(w_loaded, -2 * 16 * NW)
                act.sem_inc(wv_turned, -2)
                act.sem_inc(wvo_ready, -2)
            for s in (*plain_stored, wvo_stored):
                act.wait_ge(s, 16)

        @block.gpsimd
        def _(pool):
            for s in rot_stored:
                pool.sem_inc(s, 16)
            pool.wait_ge(w_hi_ready, 1)
            pool.sem_inc(w_hi_ready, -1)
            split_lo(0)
            with pool.Fori(0, PAIRS // 2) as i:
                for j in range(2):
                    for c in range(NC):
                        for g in range(2):
                            pool.wait_ge(multiplied, PER_PAIR * j + 2 * c + g + 1)
                            pool.wait_ge(rot_stored[g], 16)
                            pool.sem_inc(rot_stored[g], -16)
                            nc.gpsimd.tensor_tensor(rot_out[:, g, :], by_cos[:, g, :], by_sin[:, g, :],
                                                    ALU.add).then_inc(rot_done, 1)
                        if c == 1:
                            pool.wait_ge(w_hi_ready, j + 1)
                            split_lo(1 - j)
                pool.sem_inc(multiplied, -2 * PER_PAIR)
                pool.sem_inc(w_hi_ready, -2)
            for s in rot_stored:
                pool.wait_ge(s, 16)

        @block.vector
        def _(dve):
            dve.wait_ge(tables_loaded, 32)
            half = P // 2
            with dve.Fori(0, PAIRS // 2) as i:
                for j in range(2):
                    for c in range(NC):
                        toks = slice(c * CH, (c + 1) * CH)
                        for g in range(2):
                            dve.wait_ge(rot_ready, PER_PAIR * j + 2 * c + g + 1)
                            nc.vector.tensor_tensor(by_cos[:, g, :], ps[:, g, :], cos[:, toks], ALU.mult)
                            nc.vector.tensor_tensor(by_sin[0:half, g, :], ps[half:P, g, :],
                                                    sin[half:P, toks], ALU.mult)
                            nc.vector.tensor_tensor(by_sin[half:P, g, :], ps[0:half, g, :],
                                                    sin[0:half, toks], ALU.mult).then_inc(multiplied, 1)
                        if c == 2:
                            dve.wait_ge(wv_hi_ready, j + 1)
                            nc.vector.tensor_tensor(wvT[1][:],
                                                    ps[:, WV_BANK, 0:2 * P].rearrange("p (h n) -> p h n", h=2),
                                                    wvT[0][:].bitcast(F32), ALU.subtract).then_inc(wv_lo_ready, 1)
                dve.sem_inc(rot_ready, -2 * PER_PAIR)
                dve.sem_inc(wv_hi_ready, -2)

        @block.tensor
        def _(pe):
            pe.sem_inc(rot_bank_free, 2)
            pe.sem_inc(plain_bank_free, 2)
            with pe.Fori(0, PAIRS // 2) as i:
                for j in range(2):
                    pe.wait_ge(w_lo_ready, j + 1)

                    def product(bank, first, right, slices, toks):
                        n = 0
                        for k in range(slices):
                            for a, b in parts(0, 1):
                                mm = nc.tensor.matmul(ps[:, bank, :], w[j][a][:, first + k, :],
                                                      right[b][:, k, toks],
                                                      start=(n == 0), stop=(n == 3 * slices - 1))
                                n += 1
                        return mm

                    for c in range(NC):
                        toks = slice(c * CH, (c + 1) * CH)
                        for g in range(2):
                            n = PER_PAIR * j + 2 * c + g + 1
                            pe.wait_ge(rot_bank_free, n)
                            product(g, *ROT[g][1:2], ROT[g][2], ROT[g][3], toks).then_inc(rot_ready, 1)
                        if c == 2:
                            pe.wait_ge(w_lo_ready, j + 2)
                            for h in range(2):
                                last = nc.tensor.transpose(ps[:, WV_BANK, h * P:(h + 1) * P],
                                                           wv_raw[:, h, :], ident[:, :])
                            last.then_inc(wv_turned, 1)
                        for g in range(2):
                            n = PER_PAIR * j + 2 * c + g + 1
                            pe.wait_ge(plain_bank_free, n)
                            product(PLAIN0 + g, *PLAIN[g][1:2], PLAIN[g][2], PLAIN[g][3],
                                    toks).then_inc(plain_ready, 1)
                    pe.wait_ge(wv_lo_ready, j + 1)
                    for h in range(2):
                        for n, (a, b) in enumerate(parts(0, 1)):
                            last = nc.tensor.matmul(ps[:, WVO0 + h, :], wvT[a][:, h, :], wo[b][:, h, :],
                                                    start=(n == 0), stop=(n == 2))
                    last.then_inc(wvo_ready, 1)
                pe.sem_inc(w_lo_ready, -2)
                pe.sem_inc(rot_bank_free, -2 * PER_PAIR)
                pe.sem_inc(plain_bank_free, -2 * PER_PAIR)
                pe.sem_inc(wv_lo_ready, -2)


QCH = 256
TPU = QCH // P
UPH = T // QCH
UNITS = 2 * UPH
PIECE = 1024
SPLITS = 2 * NC + 1


def pieces(c):
    keys = (c + 1) * QCH
    return [(k, min(PIECE, keys - k)) for k in range(0, keys, PIECE)]


def attention_plan():
    steps = [(u, s) for u in range(UNITS) for s in range(u % UPH + 1)]
    first = [steps.index((u, 0)) for u in range(UNITS)]
    in_turn = {}
    for u in range(UNITS):
        n = u % UPH + 1
        for s in range(n):
            in_turn.setdefault(2 * u + 3 + (s >= (n + 1) // 2), []).append(first[u] + s)
    plan = []
    for g in range(TPU * UNITS + 4):
        todo = in_turn.get(g, [])
        score, softmax, out = [], [], []
        if g < TPU * UNITS:
            u, t = divmod(g, TPU)
            score = [("scores", u, t, p, b) for p, (_, keys) in enumerate(pieces(u % UPH))
                     for b in range(-(-keys // CH))]
        if 0 < g <= TPU * UNITS:
            u, t = divmod(g - 1, TPU)
            softmax = [("exp", u, t, p) for p in range(len(pieces(u % UPH)))]
        if g >= 5 and g % 2 == 1:
            out = [("out", (g - 5) // 2, t) for t in range(TPU)]
        if todo and todo[0] in first:
            plan.append(("turn", todo[0], *steps[todo[0]]))
        for k, n in enumerate(todo):
            if n + 1 < len(steps) and n + 1 not in first:
                plan.append(("turn", n + 1, *steps[n + 1]))
            if softmax:
                plan.append(softmax.pop(0))
            if k or len(todo) == 1:
                share = -(-len(score) // (len(todo) - k))
                plan += score[:share]
                score = score[share:]
            plan.append(("values", n, *steps[n]))
            if out:
                plan.append(out.pop(0))
            if n + 1 == len(steps) or n + 1 in first:
                plan.append(("sums", steps[n][0]))
        plan += softmax + score + out
        j, c = divmod(g // TPU, UPH)
        k = TPU * (c - 2) + g % TPU
        if j < 2 and 0 <= k < SPLITS:
            plan.append(("split", j, k))
    return plan


def attention(nc, hbm, keep):
    y, kv, ident = keep["y"], keep["kv"], keep["ident"]
    plan = attention_plan()
    tile_pieces = [(u, t, p) for u in range(UNITS) for t in range(TPU) for p in range(len(pieces(u % UPH)))]
    NPIECES = len(tile_pieces)
    NSTEPS = sum(e[0] == "values" for e in plan)
    piece_no = {x: n for n, x in enumerate(tile_pieces)}
    with ExitStack() as ctx:
        def sb(name, shape, dt=F32):
            return ctx.enter_context(nc.sbuf_tensor(name, shape, dt))

        def sem(name):
            return ctx.enter_context(nc.semaphore(name))

        k_raw, q_raw, w_raw = sb("k_raw", [P, T]), sb("q_raw", [P, T]), sb("wvo_raw", [P, D])
        k = [[sb(f"k_{n}{j}", [P, T], F32R) for n in ("hi", "lo")] for j in range(2)]
        q = [[sb(f"q_{n}{j}", [P, T], F32R) for n in ("hi", "lo")] for j in range(2)]
        w = [[sb(f"wvo_{n}{j}", [P, D], F32R) for n in ("hi", "lo")] for j in range(2)]
        probs = sb("probs", [P, 2, TPU, T])
        turned = [sb(f"turned_{n}", [P, 2, 2, QCH], F32R) for n in ("hi", "lo")]
        o = [sb(f"o_{n}", [P, 2, QCH], F32R) for n in ("hi", "lo")]
        negmax = sb("negmax", [P, 2, 2])
        bias = sb("bias", [P, 2, TPU])
        sums = sb("sums", [P, 4, TPU, 2])
        total = sb("total", [P, 2, TPU])
        share = sb("share", [P, 2, TPU])
        mask_raw = sb("mask_raw", [P, TPU, QCH])
        mask = sb("mask", [P, TPU, QCH], BF16)
        identb = sb("identb", [P, P], BF16)

        ps_scores = ctx.enter_context(nc.psum_tensor("ps_scores", [P, 2, PIECE], F32))
        ps_turn = ctx.enter_context(nc.psum_tensor("ps_turn", [P, 2, 2, QCH], F32))
        ps_o = ctx.enter_context(nc.psum_tensor("ps_o", [P, 2, D], F32))

        y_loaded = sem("y_loaded")
        mask_loaded = sem("mask_loaded")
        mask_ready = sem("mask_ready")
        k_loaded, q_loaded, w_loaded = sem("k_loaded"), sem("q_loaded"), sem("wvo_loaded")
        raw_free = sem("raw_free")
        split_hi_ready = sem("split_hi_ready")
        split_ready = sem("split_ready")
        scores_ready = sem("scores_ready")
        max_done = sem("max_done")
        bias_ready = sem("bias_ready")
        exp_done = sem("exp_done")
        turn_ready = sem("turn_ready")
        turned_hi_ready = sem("turned_hi_ready")
        turned_lo_ready = sem("turned_lo_ready")
        o_ready = sem("o_ready")
        o_hi_ready = sem("o_hi_ready")
        o_lo_ready = sem("o_lo_ready")
        out_ready = sem("out_ready")
        share_done = sem("share_done")
        out_added = sem("out_added")

        def load_head(sp, pair, head):
            pr = bass.ds(pair, 1)
            for n, raw, done in ((1, k_raw, k_loaded), (0, q_raw, q_loaded)):
                sp.dma_start(raw[0:ND, :], hbm["plainT"][n, pr, ND * head:ND * (head + 1), :]).then_inc(done, 16)
                for f in range(2):
                    r = P // 2 * f + HALF * head
                    sp.dma_start(raw[ND + HALF * f:ND + HALF * (f + 1), :],
                                 hbm["rotT"][n, pr, r:r + HALF, :]).then_inc(done, 16)
            sp.dma_start(w_raw[:], hbm["wvo"].rearrange("(q h p) n -> q h p n", h=2, p=P)[pr, head, :, :]
                         ).then_inc(w_loaded, 16)

        def split_views(j, n):
            if n == 2 * NC:
                return w_raw[:], w[j][0][:], w[j][1][:]
            raw, (hi, lo) = (k_raw, k[j]) if n < NC else (q_raw, q[j])
            cols = slice(n % NC * CH, (n % NC + 1) * CH)
            return raw[:, cols], hi[:, cols], lo[:, cols]

        def split_hi(act, j, n, heads_before):
            if n % NC == 0:
                loaded, loads = ((k_loaded, 3), (q_loaded, 3), (w_loaded, 1))[n // NC]
                act.wait_ge(loaded, 16 * loads * (heads_before + 1))
            raw, hi, _ = split_views(j, n)
            nc.scalar.copy(hi, raw).then_inc(split_hi_ready, 1)

        def split_lo(pool, j, n, before):
            pool.wait_ge(split_hi_ready, before + n + 1)
            raw, hi, lo = split_views(j, n)
            nc.gpsimd.tensor_tensor(lo, raw, hi.bitcast(F32), ALU.subtract).then_inc(split_ready, 1)

        block = ctx.enter_context(nc.Block())

        @block.sync
        def _(sp):
            sp.dma_start(mask_raw[:], hbm["mask"]).then_inc(mask_loaded, 16)
            load_head(sp, 0, 0)
            for m in range(4):
                sp.dma_start(y[:, 4 * m:4 * m + 4, :],
                             hbm["x"].rearrange("(t p) d -> p t d", p=P)[:, 4 * m:4 * m + 4, :]
                             ).then_inc(y_loaded, 16)
            with sp.Fori(0, PAIRS) as i:
                for j in range(2):
                    sp.wait_ge(raw_free, j + 1)
                    load_head(sp, i if j == 0 else sp.snap((i + 1) % PAIRS), 1 - j)
                sp.sem_inc(raw_free, -2)

        @block.gpsimd
        def _(pool):
            for n in range(SPLITS):
                split_lo(pool, 0, n, 0)
            pool.sem_inc(split_hi_ready, -SPLITS)
            pool.drain().then_inc(raw_free, 1)
            with pool.Fori(0, PAIRS) as i:
                for j in range(2):
                    for n in range(SPLITS):
                        split_lo(pool, 1 - j, n, SPLITS * j)
                    pool.drain().then_inc(raw_free, 1)
                pool.sem_inc(split_hi_ready, -2 * SPLITS)

        @block.scalar
        def _(act):
            act.wait_ge(mask_loaded, 16)
            nc.scalar.copy(mask[:], mask_raw[:])
            nc.scalar.copy(identb[:], ident[:]).then_inc(mask_ready, 1)
            for n in range(SPLITS):
                split_hi(act, 0, n, 0)
            act.sem_inc(k_loaded, -48)
            act.sem_inc(q_loaded, -48)
            act.sem_inc(w_loaded, -16)
            with act.Fori(0, PAIRS) as i:
                for kind, *args in plan:
                    if kind == "split":
                        j, n = args
                        split_hi(act, 1 - j, n, j)
                    if kind == "exp":
                        u, t, p = args
                        n = piece_no[u, t, p]
                        first_key, keys = pieces(u % UPH)[p]
                        act.wait_ge(bias_ready, TPU * u + t + 1)
                        nc.scalar.activation(probs[:, u % 2, t, first_key:first_key + keys],
                                             ps_scores[:, n % 2, 0:keys], ACT.Exp,
                                             bias=bias[:, u % 2, t:t + 1], scale=SCALE,
                                             accum_out=sums[:, u % 4, t, p:p + 1]).then_inc(exp_done, 1)
                    if kind == "turn":
                        n, u, s = args
                        act.wait_ge(turn_ready, n + 1)
                        nc.scalar.copy(turned[0][:, n % 2], ps_turn[:, n % 2]).then_inc(turned_hi_ready, 1)
                    if kind == "sums":
                        u, = args
                        act.wait_ge(o_ready, u + 1)
                        nc.scalar.copy(o[0][:, u % 2, :], ps_o[:, u % 2, 0:QCH]).then_inc(o_hi_ready, 1)
                act.sem_inc(k_loaded, -96)
                act.sem_inc(q_loaded, -96)
                act.sem_inc(w_loaded, -32)
                act.sem_inc(bias_ready, -TPU * UNITS)
                act.sem_inc(turn_ready, -NSTEPS)
                act.sem_inc(o_ready, -UNITS)

        @block.vector
        def _(dve):
            dve.wait_ge(y_loaded, 64)
            with dve.Fori(0, PAIRS) as i:
                for kind, *args in plan:
                    if kind == "scores":
                        u, t, p, b = args
                        tile = pieces(u % UPH)
                        keys = tile[p][1]
                        if (b + 1) * CH < keys:
                            continue
                        n = piece_no[u, t, p]
                        g = (TPU * u + t) % 2
                        dve.wait_ge(scores_ready, n + 1)
                        nc.vector.tensor_reduce(negmax[:, g, p:p + 1], ps_scores[:, n % 2, 0:keys], AX_X, ALU.max,
                                                negate=True).then_inc(max_done, 1)
                        if p + 1 < len(tile):
                            continue
                        dve.wait_ge(max_done, n + 1)
                        if len(tile) == 1:
                            nc.vector.tensor_scalar(bias[:, u % 2, t:t + 1], negmax[:, g, 0:1], SCALE, None,
                                                    ALU.mult).then_inc(bias_ready, 1)
                        else:
                            nc.vector.tensor_scalar(bias[:, u % 2, t:t + 1], negmax[:, g, 0:1], negmax[:, g, 1:2],
                                                    SCALE, ALU.min, ALU.mult).then_inc(bias_ready, 1)
                    if kind == "turn":
                        n, u, s = args
                        dve.wait_ge(turned_hi_ready, n + 1)
                        nc.vector.tensor_tensor(turned[1][:, n % 2], ps_turn[:, n % 2],
                                                turned[0][:, n % 2].bitcast(F32),
                                                ALU.subtract).then_inc(turned_lo_ready, 1)
                    if kind == "sums":
                        u, = args
                        dve.wait_ge(o_hi_ready, u + 1)
                        nc.vector.tensor_tensor(o[1][:, u % 2, :], ps_o[:, u % 2, 0:QCH],
                                                o[0][:, u % 2, :].bitcast(F32), ALU.subtract).then_inc(o_lo_ready, 1)
                    if kind == "out":
                        u, t = args
                        dve.wait_ge(out_ready, TPU * u + t + 1)
                        if t == 0:
                            total_of = sums[:, u % 4, :, 0]
                            if len(pieces(u % UPH)) > 1:
                                nc.vector.tensor_tensor(total[:, u % 2, :], sums[:, u % 4, :, 0], sums[:, u % 4, :, 1],
                                                        ALU.add).then_inc(share_done, 1)
                                total_of = total[:, u % 2, :]
                            else:
                                nc.vector.tensor_copy(total[:, u % 2, :], total_of).then_inc(share_done, 1)
                            dve.wait_ge(share_done, 2 * u + 1)
                            nc.vector.reciprocal(share[:, u % 2, :], total[:, u % 2, :]).then_inc(share_done, 1)
                            dve.wait_ge(share_done, 2 * u + 2)
                        row = TPU * (u % UPH) + t
                        nc.vector.scalar_tensor_tensor(y[:, row, :], ps_o[:, u % 2, :], share[:, u % 2, t:t + 1], y[:, row, :],
                                                       ALU.mult, ALU.add).then_inc(out_added, 1)
                dve.sem_inc(scores_ready, -NPIECES)
                dve.sem_inc(max_done, -NPIECES)
                dve.sem_inc(turned_hi_ready, -NSTEPS)
                dve.sem_inc(o_hi_ready, -UNITS)
                dve.sem_inc(out_ready, -TPU * UNITS)
                dve.sem_inc(share_done, -2 * UNITS)

        @block.tensor
        def _(pe):
            pe.wait_ge(mask_ready, 1)
            pe.sem_inc(exp_done, 2)
            pe.sem_inc(turned_lo_ready, 2)
            pe.sem_inc(out_added, 1)
            with pe.Fori(0, PAIRS) as i:
                for kind, *args in plan:
                    if kind == "scores":
                        u, t, p, b = args
                        j, c = divmod(u, UPH)
                        n = piece_no[u, t, p]
                        first_key, keys = pieces(c)[p]
                        row = TPU * c + t
                        if (c, t, p, b) == (0, 0, 0, 0):
                            pe.wait_ge(split_ready, SPLITS * (j + 1))
                        if b == 0:
                            pe.wait_ge(exp_done, n + 1)
                        k0, k1 = b * CH, min((b + 1) * CH, keys)
                        diagonal = first_key + k1 == (c + 1) * QCH
                        for m, (x, z) in enumerate(parts(0, 1)):
                            last = nc.tensor.matmul(ps_scores[:, n % 2, k0:k1], q[j][x][:, row * P:(row + 1) * P],
                                                    k[j][z][:, first_key + k0:first_key + k1],
                                                    start=(m == 0), stop=(m == 2 and not diagonal))
                        if diagonal:
                            last = nc.tensor.matmul(ps_scores[:, n % 2, k1 - QCH:k1], identb[:], mask[:, t, :],
                                                    start=False, stop=True)
                        if k1 == keys:
                            last.then_inc(scores_ready, 1)
                    if kind == "turn":
                        n, u, s = args
                        if s == 0:
                            pe.wait_ge(exp_done, 2 + piece_no[u, TPU - 1, len(pieces(u % UPH)) - 1] + 1)
                        pe.wait_ge(turned_lo_ready, n + 1)
                        for kb in range(2):
                            for t in range(TPU):
                                key = (2 * s + kb) * P
                                last = nc.tensor.transpose(ps_turn[:, n % 2, kb, t * P:(t + 1) * P],
                                                           probs[:, u % 2, t, key:key + P], ident[:])
                        last.then_inc(turn_ready, 1)
                    if kind == "values":
                        n, u, s = args
                        pe.wait_ge(turned_lo_ready, 2 + n + 1)
                        if s == 0:
                            pe.wait_ge(out_added, 1 + max(TPU * (u - 1), 0))
                        m, count = 0, 3 * 2
                        for kb in range(2):
                            for x, z in parts(0, 1):
                                last = nc.tensor.matmul(ps_o[:, u % 2, 0:QCH], kv[x][:, 2 * s + kb, :],
                                                        turned[z][:, n % 2, kb, :],
                                                        start=(s == 0 and m == 0),
                                                        stop=(s == u % UPH and m == count - 1))
                                m += 1
                        if s == u % UPH:
                            last.then_inc(o_ready, 1)
                    if kind == "out":
                        u, t = args
                        if t == 0:
                            pe.wait_ge(o_lo_ready, u + 1)
                        pe.wait_ge(out_added, TPU * u + t + 1)
                        for m, (x, z) in enumerate(parts(0, 1)):
                            last = nc.tensor.matmul(ps_o[:, u % 2, :], o[x][:, u % 2, t * P:(t + 1) * P], w[u // UPH][z][:],
                                                    start=(m == 0), stop=(m == 2))
                        last.then_inc(out_ready, 1)
                pe.sem_inc(split_ready, -2 * SPLITS)
                pe.sem_inc(exp_done, -NPIECES)
                pe.sem_inc(turned_lo_ready, -NSTEPS)
                pe.sem_inc(o_lo_ready, -UNITS)
                pe.sem_inc(out_added, -TPU * UNITS)


ET = E // P
QUARTERS = 4


def ternary_weights(nc, hbm, keep, ffn):
    y, ident = keep["y"], keep["ident"]
    wT, scale, mv, rstd = ffn["wT"], ffn["scale"], ffn["mv"], ffn["rstd"]
    QW = D * E // P // QUARTERS
    sources = (hbm["W_up"].rearrange("(r p) n -> p r n", p=P),
               hbm["W_gate"].rearrange("(r p) n -> p r n", p=P),
               hbm["W_down"].rearrange("(r p) n -> p r n", p=P))
    with ExitStack() as ctx:
        def sb(name, shape, dt=F32):
            return ctx.enter_context(nc.sbuf_tensor(name, shape, dt))

        def sem(name):
            return ctx.enter_context(nc.semaphore(name))

        raw = [sb(f"ternary_raw{m}", [P, QUARTERS, QW]) for m in range(2)]
        signs = sb("signs", [P, 2, QW], BF16)
        abs_sums = sb("abs_sums", [P, 3, QUARTERS])
        total = sb("abs_total", [P, 3])
        bound = sb("bound", [P, 3, 2])
        ones = sb("ones", [P, P])
        identb = sb("identb3", [P, P], BF16)
        bn = sb("bn3", [P, 2, 6])
        std = sb("std3", [P, NT])
        ps_turn = ctx.enter_context(nc.psum_tensor("ps_signs", [P, 4, 2 * CH], BF16))
        ps_sum = ctx.enter_context(nc.psum_tensor("ps_abs", [P, CH], F32))

        loaded = [[sem(f"ternary_loaded{b}{q}") for q in range(QUARTERS)] for b in range(2)]
        ones_ready = sem("ones_ready")
        identb_ready = sem("identb_ready")
        stats_done = sem("stats3_done")
        var_ready = sem("var3_ready")
        std_ready = sem("std3_ready")
        abs_ready = sem("abs_ready")
        abs_summed = sem("abs_summed")
        scale_done = sem("scale_done")
        below_done = sem("below_done")
        signs_ready = sem("signs_ready")
        signs_turned = sem("signs_turned")
        signs_copied = sem("signs_copied")
        signs_free = sem("signs_free")
        raw_free = sem("ternary_raw_free")

        block = ctx.enter_context(nc.Block())

        @block.sync
        def _(sp):
            for m in range(3):
                for q in range(QUARTERS):
                    if m == 2:
                        sp.wait_ge(raw_free, q + 1)
                    n = (ET if m < 2 else KD) // QUARTERS
                    sp.dma_start(raw[m % 2][:, q, :].rearrange("p (r n) -> p r n", r=n),
                                 sources[m][:, n * q:n * (q + 1), :]).then_inc(loaded[m % 2][q], 16)

        @block.gpsimd
        def _(pool):
            nc.gpsimd.memset(ones[:], 1.0).then_inc(ones_ready, 1)

        @block.scalar
        def _(act):
            nc.scalar.copy(identb[:], ident[:]).then_inc(identb_ready, 1)
            act.wait_ge(var_ready, 1)
            nc.scalar.activation(std[:], std[:], ACT.Sqrt).then_inc(std_ready, 1)

            def abs_sum(m, q):
                act.wait_ge(loaded[m % 2][q], 16 * (m // 2 + 1))
                unused = (wT[1][:, q, :] if m == 1 else
                          wT[2][:, QW // D * q:QW // D * (q + 1), :].rearrange("p r n -> p (r n)"))
                nc.scalar.activation(unused, raw[m % 2][:, q, :], ACT.Abs,
                                     accum_out=abs_sums[:, m, q:q + 1]).then_inc(abs_ready, 1)

            for q in range(QUARTERS):
                abs_sum(0, q)
            for m in range(3):
                for q in range(QUARTERS):
                    if m < 2:
                        abs_sum(m + 1, q)
                    for b in range(4):
                        act.wait_ge(signs_turned, 16 * m + 4 * q + b + 1)
                        turned = ps_turn[:, b, 0:CH]
                        if m < 2:
                            put = wT[m][:, b, q * CH:(q + 1) * CH]
                        else:
                            put = wT[m][:, 4 * b:4 * b + 4, q * P:(q + 1) * P]
                            turned = turned.rearrange("p (e n) -> p e n", e=4)
                        nc.scalar.copy(put, turned).then_inc(signs_copied, 1)
                    act.sem_inc(signs_free, 1)
                    if m == 0:
                        act.sem_inc(raw_free, 1)

        @block.vector
        def _(dve):
            for t in range(NT):
                nc.vector.bn_stats(bn[:, t % 2, :], y[:, t, :]).then_inc(stats_done, 1)
                dve.wait_ge(stats_done, 2 * t + 1)
                nc.vector.bn_aggr(mv[:, t, :], bn[:, t % 2, :]).then_inc(stats_done, 1)
            dve.wait_ge(stats_done, 2 * NT)
            nc.vector.tensor_scalar(std[:], mv[:, :, 1], LN_EPS, None, ALU.add).then_inc(var_ready, 1)
            dve.wait_ge(std_ready, 1)
            nc.vector.reciprocal(rstd[:], std[:])
            for m in range(3):
                dve.wait_ge(abs_summed, m + 1)
                nc.vector.tensor_reduce(total[:, m:m + 1], ps_sum[:, 4 * m:4 * m + 4], AX_X, ALU.add
                                        ).then_inc(scale_done, 1)
                dve.wait_ge(scale_done, 3 * m + 1)
                nc.vector.tensor_scalar(scale[:, m:m + 1], total[:, m:m + 1], 1.0 / (D * E), QUANT_EPS,
                                        ALU.mult, ALU.add).then_inc(scale_done, 1)
                dve.wait_ge(scale_done, 3 * m + 2)
                nc.vector.tensor_scalar(bound[:, m, 0:1], scale[:, m:m + 1], 0.5, None, ALU.mult)
                nc.vector.tensor_scalar(bound[:, m, 1:2], scale[:, m:m + 1], -0.5, None, ALU.mult
                                        ).then_inc(scale_done, 1)
                dve.wait_ge(scale_done, 3 * m + 3)
                for q in range(QUARTERS):
                    n = QUARTERS * m + q
                    if n >= 2:
                        dve.wait_ge(signs_free, n - 1)
                    below = signs[:, n % 2, :]
                    nc.vector.tensor_scalar(below, raw[m % 2][:, q, :], bound[:, m, 1:2], None,
                                            ALU.is_lt).then_inc(below_done, 1)
                    dve.wait_ge(below_done, n + 1)
                    nc.vector.scalar_tensor_tensor(signs[:, n % 2, :], raw[m % 2][:, q, :], bound[:, m, 0:1], below,
                                                   ALU.is_gt, ALU.subtract).then_inc(signs_ready, 1)

        @block.tensor
        def _(pe):
            pe.wait_ge(ones_ready, 1)
            pe.wait_ge(identb_ready, 1)
            for m in range(3):
                pe.wait_ge(abs_ready, QUARTERS * (m + 1))
                nc.tensor.matmul(ps_sum[:, 4 * m:4 * m + 4], ones[:], abs_sums[:, m, :],
                                 start=True, stop=True).then_inc(abs_summed, 1)
                for q in range(QUARTERS):
                    n = QUARTERS * m + q
                    pe.wait_ge(signs_ready, n + 1)
                    for b in range(4):
                        if n:
                            pe.wait_ge(signs_copied, 4 * (n - 1) + b + 1)
                        for r in range(4):
                            at = (r * D + b * P) if m < 2 else (4 * b + r) * P
                            last = nc.tensor.transpose(ps_turn[:, b, r * P:(r + 1) * P],
                                                       signs[:, n % 2, at:at + P], identb[:])
                        last.then_inc(signs_turned, 1)


def feed_forward(nc, hbm, keep, ffn, out):
    y, ident = keep["y"], keep["ident"]
    wT, scale, mv, rstd = ffn["wT"], ffn["scale"], ffn["mv"], ffn["rstd"]
    UP, GATE, DOWN = range(3)
    TC = CH // P
    NORM_AT = {2 + 3 * t: t for t in range(TC)}
    with ExitStack() as ctx:
        def sb(name, shape, dt=F32):
            return ctx.enter_context(nc.sbuf_tensor(name, shape, dt))

        def sem(name):
            return ctx.enter_context(nc.semaphore(name))

        xn = sb("xn3", [P, 2, D])
        hT = [sb(f"hT_{n}", [P, 2, KD, CH], F32R) for n in ("hi", "lo")]
        gated = sb("gated", [P, CH])
        hidden = sb("hidden", [P, CH])
        hid = [sb(f"hidden_{n}", [P, 2, CH], F32R) for n in ("hi", "lo")]
        result = sb("result", [P, TC, D])
        ps_acc = ctx.enter_context(nc.psum_tensor("ps_acc", [P, TC, D], F32))
        ps_up = ctx.enter_context(nc.psum_tensor("ps_up", [P, 2, CH], F32))
        ps_gate = ctx.enter_context(nc.psum_tensor("ps_gate", [P, CH], F32))
        ps_turn = ctx.enter_context(nc.psum_tensor("ps_turn3", [P, D], F32))

        xn_ready = sem("xn3_ready")
        turn_ready = sem("turn3_ready")
        h_hi_ready = sem("h_hi_ready")
        h_lo_ready = sem("h_lo_ready")
        up_ready = sem("up_ready")
        silu_ready = sem("silu_ready")
        gate_ready = sem("gate_ready")
        hidden_ready = sem("hidden_ready")
        hid_hi_ready = sem("hid_hi_ready")
        hid_lo_ready = sem("hid_lo_ready")
        acc_ready = sem("acc_ready")
        result_ready = sem("result_ready")
        acc_free = sem("acc_free")
        stored = [sem(f"stored{t}") for t in range(TC)]

        block = ctx.enter_context(nc.Block())

        def h_tile(part, slot, t):
            return hT[part][:, bass.ds(slot, 1), :, t * P:(t + 1) * P]

        def turned():
            return ps_turn[:].rearrange("p (k n) -> p k n", k=KD)

        @block.vector
        def _(dve):
            def normalise(chunk, t):
                row = bass.ds(chunk * TC + t, 1)
                nc.vector.tensor_scalar(xn[:, t % 2, :], y[:, row, :], mv[:, row, 0], rstd[:, row],
                                        ALU.subtract, ALU.mult).then_inc(xn_ready, 1)

            def h_low(slot, t, count):
                dve.wait_ge(h_hi_ready, count)
                nc.vector.tensor_tensor(h_tile(1, slot, t), turned(), h_tile(0, slot, t).bitcast(F32),
                                        ALU.subtract).then_inc(h_lo_ready, 1)

            for t in range(TC):
                normalise(0, t)
                h_low(0, t, t + 1)
            dve.sem_inc(h_hi_ready, -TC)
            for s in stored:
                dve.sem_inc(s, 16)
            with dve.Fori(0, NC) as i:
                following, slot = dve.snap((i + 1) % NC), dve.snap((i + 1) % 2)
                for e in range(ET):
                    if e in NORM_AT:
                        normalise(following, NORM_AT[e])
                    dve.wait_ge(silu_ready, e + 1)
                    dve.wait_ge(gate_ready, e + 1)
                    nc.vector.scalar_tensor_tensor(hidden[:], ps_gate[:], scale[:, GATE:GATE + 1], gated[:],
                                                   ALU.mult, ALU.mult).then_inc(hidden_ready, 1)
                    dve.wait_ge(hid_hi_ready, e + 1)
                    nc.vector.tensor_tensor(hid[1][:, e % 2, :], hidden[:], hid[0][:, e % 2, :].bitcast(F32),
                                            ALU.subtract).then_inc(hid_lo_ready, 1)
                    if e in NORM_AT:
                        h_low(slot, NORM_AT[e], NORM_AT[e] + 1)
                for t in range(TC):
                    dve.wait_ge(acc_ready, t + 1)
                    dve.wait_ge(stored[t], 16)
                    dve.sem_inc(stored[t], -16)
                    nc.vector.scalar_tensor_tensor(result[:, t, :], ps_acc[:, t, :], scale[:, DOWN:DOWN + 1],
                                                   y[:, bass.ds(i * TC + t, 1), :].rearrange("p a n -> p (a n)"),
                                                   ALU.mult, ALU.add).then_inc(result_ready, 1)
                dve.sem_inc(silu_ready, -ET)
                dve.sem_inc(gate_ready, -ET)
                dve.sem_inc(hid_hi_ready, -ET)
                dve.sem_inc(h_hi_ready, -TC)
                dve.sem_inc(acc_ready, -TC)
            for s in stored:
                dve.wait_ge(s, 16)

        @block.sync
        def _(sp):
            with sp.Fori(0, NC) as i:
                for t in range(TC):
                    sp.wait_ge(result_ready, t + 1)
                    sp.sem_inc(acc_free, 1)
                    sp.dma_start(out.rearrange("(t p) d -> t p d", p=P)[bass.ds(i * TC + t, 1), :, :],
                                 result[:, t, :]).then_inc(stored[t], 16)
                sp.sem_inc(result_ready, -TC)

        @block.scalar
        def _(act):
            def h_high(slot, t, count):
                act.wait_ge(turn_ready, count)
                nc.scalar.copy(h_tile(0, slot, t), turned()).then_inc(h_hi_ready, 1)

            for t in range(TC):
                h_high(0, t, t + 1)
            act.sem_inc(turn_ready, -TC)
            with act.Fori(0, NC) as i:
                slot = act.snap((i + 1) % 2)
                for e in range(ET):
                    act.wait_ge(up_ready, e + 1)
                    nc.scalar.activation(gated[:], ps_up[:, e % 2, :], ACT.Silu, scale=scale[:, UP:UP + 1]
                                         ).then_inc(silu_ready, 1)
                    act.wait_ge(hidden_ready, e + 1)
                    nc.scalar.copy(hid[0][:, e % 2, :], hidden[:]).then_inc(hid_hi_ready, 1)
                    if e in NORM_AT:
                        h_high(slot, NORM_AT[e], NORM_AT[e] + 1)
                act.sem_inc(up_ready, -ET)
                act.sem_inc(hidden_ready, -ET)
                act.sem_inc(turn_ready, -TC)

        @block.tensor
        def _(pe):
            def turn(t):
                pe.wait_ge(xn_ready, t + 1)
                for k in range(KD):
                    last = nc.tensor.transpose(ps_turn[:, k * P:(k + 1) * P],
                                               xn[:, t % 2, k * P:(k + 1) * P], ident[:])
                last.then_inc(turn_ready, 1)

            def down(e):
                pe.wait_ge(hid_lo_ready, e + 1)
                for t in range(TC):
                    if e == 0:
                        pe.wait_ge(acc_free, t + 1)
                    for part in range(2):
                        last = nc.tensor.matmul(ps_acc[:, t, :], hid[part][:, e % 2, t * P:(t + 1) * P],
                                                wT[DOWN][:, e, :], start=(e == 0 and part == 0),
                                                stop=(e == ET - 1 and part == 1))
                    if e == ET - 1:
                        last.then_inc(acc_ready, 1)

            for t in range(TC):
                turn(t)
            pe.sem_inc(xn_ready, -TC)
            pe.sem_inc(acc_free, TC)
            with pe.Fori(0, NC) as i:
                slot = pe.snap(i % 2)
                pe.wait_ge(h_lo_ready, TC)
                for e in range(ET):
                    for m, bank, ready in ((UP, ps_up[:, e % 2, :], up_ready), (GATE, ps_gate[:], gate_ready)):
                        before = e - 1 if m == UP else e
                        if before > 0:
                            pe.wait_ge(hid_lo_ready, before)
                        for kk in range(KD):
                            for part in range(2):
                                last = nc.tensor.matmul(bank, wT[m][:, kk, e * P:(e + 1) * P],
                                                        hT[part][:, bass.ds(slot, 1), kk, :],
                                                        start=(kk == 0 and part == 0),
                                                        stop=(kk == KD - 1 and part == 1))
                        last.then_inc(ready, 1)
                    if e:
                        down(e - 1)
                    if e in NORM_AT:
                        turn(NORM_AT[e])
                down(ET - 1)
                pe.sem_inc(h_lo_ready, -TC)
                pe.sem_inc(hid_lo_ready, -ET)
                pe.sem_inc(acc_free, -TC)
                pe.sem_inc(xn_ready, -TC)


def program(nc, hbm, out):
    hbm["plainT"] = nc.dram_tensor("plainT", [2, PAIRS, P, T], F32, kind="Internal").ap()
    hbm["rotT"] = nc.dram_tensor("rotT", [2, PAIRS, P, T], F32, kind="Internal").ap()
    hbm["wvo"] = nc.dram_tensor("wvo", [H * P, D], F32, kind="Internal").ap()

    def sb(owner, name, shape, dt=F32):
        return owner.enter_context(nc.sbuf_tensor(name, shape, dt))

    def two(owner, name, shape):
        return [sb(owner, f"{name}_{n}", shape, F32R) for n in ("hi", "lo")]

    with ExitStack() as ctx:
        keep = {"ident": sb(ctx, "ident", [P, P])}
        place = nc.sbuf_base
        keep["y"] = sb(ctx, "y", [P, NT, D])
        qlatT = [nc.alloc_sbuf_tensor_at(f"qlatT_{n}", [P, KQ, T], F32R, offset=place + i * KQ * T * 4)
                 for i, n in enumerate(("hi", "lo"))]
        with ExitStack() as c1:
            keep["kv"] = two(c1, "kv", [P, NT, KVR])
            with ExitStack() as c2:
                xT, kvT = two(c2, "xT", [P, KD, T]), two(c2, "kvT", [P, T])
                latents(nc, hbm, keep, xT, qlatT, kvT)
                heads_inputs(nc, hbm, keep, xT, qlatT, kvT)
            attention(nc, hbm, keep)
        ffn = {"wT": [sb(ctx, f"wT_{n}", shape, F32R) for n, shape in
                      (("up", [P, KD, E]), ("gate", [P, KD, E]), ("down", [P, ET, D]))],
               "scale": sb(ctx, "scale", [P, 3]), "mv": sb(ctx, "mv3", [P, NT, 2]), "rstd": sb(ctx, "rstd3", [P, NT])}
        ternary_weights(nc, hbm, keep, ffn)
        feed_forward(nc, hbm, keep, ffn, out)


def constants():
    freq = (np.float32(1.0) / np.power(np.float32(ROPE_BASE), np.arange(HALF, dtype=np.float32) / np.float32(HALF)))
    angle = (np.arange(T, dtype=np.float32)[:, None] * freq.astype(np.float32)).T
    cos = np.tile(np.cos(angle).astype(np.float32), (4, 1))
    sin = np.tile(np.sin(angle).astype(np.float32), (4, 1))
    sin[P // 2:] *= np.float32(-1.0)
    query = np.arange(QCH).reshape(TPU, P).T[:, :, None]
    mask = np.where(np.arange(QCH)[None, None, :] > query, np.float32(NEG), np.float32(0.0)).astype(np.float32)
    return {"ident": np.eye(P, dtype=np.float32), "mask": mask, "cos": cos, "sin": sin}


NAMES = ("x", "Wq_down", "Wq_up", "Wq_rope", "Wkv_down", "Wk_up", "Wk_rope", "Wv_up", "Wo", "W_up", "W_gate", "W_down")


def kernel(**inputs):
    import concourse.bacc as bacc
    from concourse.bass_utils import run_bass_kernel_spmd

    nc = bacc.Bacc("TRN2", target_bir_lowering=False, num_devices=1)
    arrays = {}
    for name in NAMES:
        a = np.ascontiguousarray(inputs[f"L0_{'ffn' if name in ('W_up', 'W_gate', 'W_down') else 'attn'}_{name}"])
        arrays[name] = a.reshape(T, D) if name == "x" else a
    arrays.update(constants())
    hbm = {n: nc.dram_tensor(f"in_{n}", a.shape, mybir.dt.from_np(a.dtype), kind="ExternalInput").ap()
           for n, a in arrays.items()}
    out = nc.dram_tensor("out", [T, D], F32, kind="ExternalOutput").ap()
    program(nc, hbm, out)
    r = run_bass_kernel_spmd(nc, [{f"in_{n}": a for n, a in arrays.items()}], core_ids=[0])
    return r.results[0]["out"].reshape(1, T, D)
```

```python
from contextlib import ExitStack

import numpy as np

import concourse.bass as bass
from concourse import mybir

ALU = mybir.AluOpType
ACT = mybir.ActivationFunctionType
AX_X = mybir.AxisListType.X
F32 = mybir.dt.float32
F32R = mybir.dt.float32r
BF16 = mybir.dt.bfloat16

P = 128
LN_EPS = 1e-5
QUANT_EPS = 1e-8
NEG = -1e30
ROPE_BASE = 10000.0

T, D = 2048, 512
H, HD, RD = 16, 128, 64
HALF = RD // 2
ND = HD - RD
QR, KVR = 256, 128
E = 2048
KD = D // P
KQ = QR // P
NT = T // P
CH = 512
NC = T // CH
TC = CH // P
PAIRS = H // 2
SCALE = float(HD) ** -0.5


def parts(hi, lo):
    return ((hi, hi), (hi, lo), (lo, hi))


def latents(nc, hbm, keep, xT, qlatT, kvT):
    ident, kv = keep["ident"], keep["kv"]
    NL = KQ + 1
    LAT0 = 2
    with ExitStack() as ctx:
        def sb(name, shape, dt=F32):
            return ctx.enter_context(nc.sbuf_tensor(name, shape, dt))

        def sem(name):
            return ctx.enter_context(nc.semaphore(name))

        x = sb("x", [P, NT, D])
        w_raw = sb("wlat_raw", [P, KD, QR + KVR])
        w = [sb(f"wlat_{n}", [P, KD, QR + KVR], F32R) for n in ("hi", "lo")]
        bn = sb("bn", [P, TC, 6])
        mv = sb("mv", [P, NT, 2])
        std = sb("std", [P, NT])
        rstd = sb("rstd", [P, NT])
        xn = sb("xn", [P, TC, D])
        ps = ctx.enter_context(nc.psum_tensor("ps_lat", [P, 8, CH], F32))

        ident_loaded = sem("ident_loaded")
        x_loaded = [sem(f"x_loaded{i}") for i in range(NC)]
        wlat_loaded = sem("wlat_loaded")
        stats_done = sem("stats_done")
        var_ready = sem("var_ready")
        std_ready = sem("std_ready")
        rstd_done = sem("rstd_done")
        xn_ready = sem("xn_ready")
        xt_ready = sem("xt_ready")
        xt_hi_ready = sem("xt_hi_ready")
        xt_lo_ready = sem("xt_lo_ready")
        wlat_hi_ready = sem("wlat_hi_ready")
        wlat_lo_ready = sem("wlat_lo_ready")
        lat_ready = sem("lat_ready")
        lat_hi_ready = sem("lat_hi_ready")
        lat_lo_ready = sem("lat_lo_ready")
        kv_hi_turned = sem("kv_hi_turned")
        kv_lo_turned = sem("kv_lo_turned")

        def lat(dst, m, c):
            cols = slice(c * CH, (c + 1) * CH)
            return qlatT[dst][:, m, cols] if m < KQ else kvT[dst][:, cols]

        def lat_scale(m):
            return SCALE if m < KQ else 1.0

        block = ctx.enter_context(nc.Block())

        @block.sync
        def _(sp):
            sp.dma_start(ident[:], hbm["ident"]).then_inc(ident_loaded, 16)
            for c in range(NC):
                rows = slice(TC * c, TC * (c + 1))
                sp.dma_start(x[:, rows, :], hbm["x"].rearrange("(t p) d -> p t d", p=P)[:, rows, :]
                             ).then_inc(x_loaded[c], 16)
                if c == 0:
                    sp.dma_start(w_raw[:, :, 0:QR],
                                 hbm["Wq_down"].rearrange("(k p) n -> p k n", p=P)).then_inc(wlat_loaded, 16)
                    sp.dma_start(w_raw[:, :, QR:QR + KVR],
                                 hbm["Wkv_down"].rearrange("(k p) n -> p k n", p=P)).then_inc(wlat_loaded, 16)

        @block.vector
        def _(dve):
            dve.wait_ge(wlat_hi_ready, 1)
            nc.vector.tensor_tensor(w[1][:], w_raw[:], w[0][:].bitcast(F32),
                                    ALU.subtract).then_inc(wlat_lo_ready, 1)

            def normalise(c):
                tiles = range(TC * c, TC * (c + 1))
                dve.wait_ge(x_loaded[c], 16)
                for t in tiles:
                    nc.vector.bn_stats(bn[:, t % TC, :], x[:, t, :]).then_inc(stats_done, 1)
                for t in tiles:
                    dve.wait_ge(stats_done, TC * 2 * c + t % TC + 1)
                    nc.vector.bn_aggr(mv[:, t, :], bn[:, t % TC, :]).then_inc(stats_done, 1)
                dve.wait_ge(stats_done, TC * 2 * (c + 1))
                rows = slice(TC * c, TC * (c + 1))
                nc.vector.tensor_scalar(std[:, rows], mv[:, rows, 1], LN_EPS, None, ALU.add).then_inc(var_ready, 1)
                dve.wait_ge(std_ready, c + 1)
                nc.vector.reciprocal(rstd[:, rows], std[:, rows]).then_inc(rstd_done, 1)
                dve.wait_ge(rstd_done, c + 1)
                for t in tiles:
                    nc.vector.tensor_scalar(xn[:, t % TC, :], x[:, t, :], mv[:, t, 0:1], rstd[:, t:t + 1],
                                            ALU.subtract, ALU.mult).then_inc(xn_ready, 1)

            def x_low(c):
                for t in range(TC * c, TC * (c + 1)):
                    dve.wait_ge(xt_hi_ready, t + 1)
                    nc.vector.tensor_tensor(xT[1][:, :, t * P:(t + 1) * P],
                                            ps[:, t % 2, :].rearrange("p (k n) -> p k n", k=KD),
                                            xT[0][:, :, t * P:(t + 1) * P].bitcast(F32),
                                            ALU.subtract).then_inc(xt_lo_ready, 1)

            def latent_low(c):
                for m in range(NL):
                    dve.wait_ge(lat_hi_ready, NL * c + m + 1)
                    nc.vector.scalar_tensor_tensor(lat(1, m, c), ps[:, LAT0 + m, :], lat_scale(m),
                                                   lat(0, m, c).bitcast(F32), ALU.mult,
                                                   ALU.subtract).then_inc(lat_lo_ready, 1)

            for c in range(NC + 1):
                if c < NC:
                    normalise(c)
                    x_low(c)
                if c:
                    latent_low(c - 1)
            for b in range(NT // 4):
                dve.wait_ge(kv_lo_turned, b + 1)
                nc.vector.tensor_copy(kv[1][:, 4 * b:4 * b + 4, :],
                                      ps[:, 4 + b, :].rearrange("p (t n) -> p t n", t=4))

        @block.scalar
        def _(act):
            act.wait_ge(wlat_loaded, 32)
            nc.scalar.copy(w[0][:], w_raw[:]).then_inc(wlat_hi_ready, 1)
            for c in range(NC + 1):
                if c < NC:
                    rows = slice(TC * c, TC * (c + 1))
                    act.wait_ge(var_ready, c + 1)
                    nc.scalar.activation(std[:, rows], std[:, rows], ACT.Sqrt).then_inc(std_ready, 1)
                    for t in range(TC * c, TC * (c + 1)):
                        act.wait_ge(xt_ready, t + 1)
                        nc.scalar.copy(xT[0][:, :, t * P:(t + 1) * P],
                                       ps[:, t % 2, :].rearrange("p (k n) -> p k n", k=KD)).then_inc(xt_hi_ready, 1)
                if c:
                    for m in range(NL):
                        act.wait_ge(lat_ready, NL * (c - 1) + m + 1)
                        nc.scalar.activation(lat(0, m, c - 1), ps[:, LAT0 + m, :], ACT.Copy,
                                             scale=lat_scale(m)).then_inc(lat_hi_ready, 1)
            for b in range(NT // 4):
                act.wait_ge(kv_hi_turned, b + 1)
                nc.scalar.copy(kv[0][:, 4 * b:4 * b + 4, :],
                               ps[:, b, :].rearrange("p (t n) -> p t n", t=4))

        @block.tensor
        def _(pe):
            pe.wait_ge(ident_loaded, 16)
            for c in range(NC + 1):
                if c < NC:
                    for t in range(TC * c, TC * (c + 1)):
                        pe.wait_ge(xn_ready, t + 1)
                        if t >= 2:
                            pe.wait_ge(xt_lo_ready, t - 1)
                        for k in range(KD):
                            last = nc.tensor.transpose(ps[:, t % 2, k * P:(k + 1) * P],
                                                       xn[:, t % TC, k * P:(k + 1) * P], ident[:, :])
                        last.then_inc(xt_ready, 1)
                if c == 0:
                    continue
                pe.wait_ge(xt_lo_ready, TC * c)
                if c == 1:
                    pe.wait_ge(wlat_lo_ready, 1)
                for m in range(NL):
                    if c > 1:
                        pe.wait_ge(lat_lo_ready, NL * (c - 2) + m + 1)
                    n = 0
                    for k in range(KD):
                        for a, b in parts(0, 1):
                            last = nc.tensor.matmul(ps[:, LAT0 + m, :], w[a][:, k, m * P:(m + 1) * P],
                                                    xT[b][:, k, (c - 1) * CH:c * CH],
                                                    start=(n == 0), stop=(n == 3 * KD - 1))
                            n += 1
                    last.then_inc(lat_ready, 1)
            pe.wait_ge(lat_lo_ready, NL * NC)
            for b in range(NT // 4):
                for part, done in ((0, kv_hi_turned), (1, kv_lo_turned)):
                    for q in range(4):
                        t = 4 * b + q
                        last = nc.tensor.transpose(ps[:, 4 * part + b, q * P:(q + 1) * P],
                                                   kvT[part][:, t * P:(t + 1) * P].bitcast(F32), ident[:, :])
                    last.then_inc(done, 1)


def heads_inputs(nc, hbm, keep, xT, qlatT, kvT):
    ident = keep["ident"]
    ROT_Q, ROT_K, PLAIN_Q, PLAIN_K = 0, KQ, KQ + KD, 2 * KQ + KD
    NSL = 2 * KQ + KD + 1
    Q, K = 0, 1
    ROT = ((K, ROT_K, xT, KD), (Q, ROT_Q, qlatT, KQ))
    PLAIN = ((Q, PLAIN_Q, qlatT, KQ), (K, PLAIN_K, [z[:].rearrange("p (k n) -> p k n", k=1) for z in kvT], 1))
    PLAIN0, WV_BANK, WVO0 = 2, 4, 5
    with ExitStack() as ctx:
        def sb(name, shape, dt=F32):
            return ctx.enter_context(nc.sbuf_tensor(name, shape, dt))

        def sem(name):
            return ctx.enter_context(nc.semaphore(name))

        cos, sin = sb("cos", [P, T]), sb("sin", [P, T])
        w_raw = sb("w_raw", [P, NSL, P])
        w = [[sb(f"w_{n}{j}", [P, NSL, P], F32R) for n in ("hi", "lo")] for j in range(2)]
        wv_raw = sb("wv_raw", [P, 2, P])
        wvT = [sb(f"wvT_{n}", [P, 2, P], F32R) for n in ("hi", "lo")]
        wo_raw = sb("wo_raw", [P, 2, D])
        wo = [sb(f"wo_{n}", [P, 2, D], F32R) for n in ("hi", "lo")]
        wvo_out = sb("wvo_out", [P, 2, D])
        by_cos = sb("by_cos", [P, 2, CH])
        by_sin = sb("by_sin", [P, 2, CH])
        rot_out = sb("rot_out", [P, 2, CH])
        plain_out = sb("plain_out", [P, 2, CH])
        ps = ctx.enter_context(nc.psum_tensor("ps_proj", [P, 8, CH], F32))

        tables_loaded = sem("tables_loaded")
        w_loaded = sem("w_loaded")
        w_hi_ready = sem("w_hi_ready")
        w_lo_ready = sem("w_lo_ready")
        wo_hi_ready = sem("wo_hi_ready")
        wv_turned = sem("wv_turned")
        wv_hi_ready = sem("wv_hi_ready")
        wv_lo_ready = sem("wv_lo_ready")
        wvo_ready = sem("wvo_ready")
        wvo_copied = sem("wvo_copied")
        wvo_stored = sem("wvo_stored")
        rot_ready = sem("rot_ready")
        rot_bank_free = sem("rot_bank_free")
        multiplied = sem("multiplied")
        rot_done = sem("rot_done")
        rot_stored = [sem(f"rot_stored{i}") for i in range(2)]
        plain_ready = sem("plain_ready")
        plain_bank_free = sem("plain_bank_free")
        plain_done = sem("plain_done")
        plain_stored = [sem(f"plain_stored{i}") for i in range(2)]

        NW = 6
        PER_PAIR = 2 * NC

        def load_weights(sp, pair):
            cols, heads = bass.ds(pair * P, P), bass.ds(pair * 2, 2)
            for name, s0, k in (("Wq_rope", ROT_Q, KQ), ("Wk_rope", ROT_K, KD),
                                ("Wq_up", PLAIN_Q, KQ), ("Wk_up", PLAIN_K, 1)):
                sp.dma_start(w_raw[:, s0:s0 + k, :],
                             hbm[name].rearrange("(k p) n -> p k n", p=P)[:, :, cols]).then_inc(w_loaded, 16)
            sp.dma_start(wv_raw[:], hbm["Wv_up"].rearrange("p (h n) -> p h n", n=P)[:, heads, :]
                         ).then_inc(w_loaded, 16)
            sp.dma_start(wo_raw[:], hbm["Wo"].rearrange("(h p) n -> p h n", p=P)[:, heads, :]
                         ).then_inc(w_loaded, 16)

        def rotary_views(j, part, f):
            raw = w_raw[:, 0:PLAIN_Q, :].rearrange("p k (h f r) -> p k f h r", h=2, f=2)[:, :, f]
            put = w[j][part][:, 0:PLAIN_Q, :].rearrange("p k (f h r) -> p k f h r", h=2, f=2)[:, :, f]
            return put, raw

        def split_hi(j):
            for f in range(2):
                put, raw = rotary_views(j, 0, f)
                nc.scalar.copy(put, raw)
            nc.scalar.copy(w[j][0][:, PLAIN_Q:NSL, :], w_raw[:, PLAIN_Q:NSL, :]).then_inc(w_hi_ready, 1)

        def split_lo(j):
            for f in range(2):
                put, raw = rotary_views(j, 1, f)
                nc.gpsimd.tensor_tensor(put, raw, rotary_views(j, 0, f)[0].bitcast(F32), ALU.subtract)
            nc.gpsimd.tensor_tensor(w[j][1][:, PLAIN_Q:NSL, :], w_raw[:, PLAIN_Q:NSL, :],
                                    w[j][0][:, PLAIN_Q:NSL, :].bitcast(F32),
                                    ALU.subtract).then_inc(w_lo_ready, 1)

        block = ctx.enter_context(nc.Block())

        @block.sync
        def _(sp):
            load_weights(sp, 0)
            sp.dma_start(cos[:], hbm["cos"]).then_inc(tables_loaded, 16)
            sp.dma_start(sin[:], hbm["sin"]).then_inc(tables_loaded, 16)
            with sp.Fori(0, PAIRS // 2) as i:
                for j in range(2):
                    pair = 2 * i + j
                    following = sp.snap((pair + 1) % PAIRS)
                    for c in range(NC):
                        toks = slice(c * CH, (c + 1) * CH)
                        for g in range(2):
                            sp.wait_ge(rot_done, PER_PAIR * j + 2 * c + g + 1)
                            sp.sem_inc(rot_bank_free, 1)
                            sp.dma_start(hbm["rotT"][ROT[g][0], bass.ds(pair, 1), :, toks],
                                         rot_out[:, g, :]).then_inc(rot_stored[g], 16)
                        for g in range(2):
                            sp.wait_ge(plain_done, PER_PAIR * j + 2 * c + g + 1)
                            sp.sem_inc(plain_bank_free, 1)
                            sp.dma_start(hbm["plainT"][PLAIN[g][0], bass.ds(pair, 1), :, toks],
                                         plain_out[:, g, :]).then_inc(plain_stored[g], 16)
                        if c == 0:
                            load_weights(sp, following)
                    sp.wait_ge(wvo_copied, j + 1)
                    sp.dma_start(hbm["wvo"].rearrange("(h p) n -> p h n", p=P)[:, bass.ds(2 * following, 2), :],
                                 wvo_out[:]).then_inc(wvo_stored, 16)
                sp.sem_inc(plain_done, -2 * PER_PAIR)
                sp.sem_inc(rot_done, -2 * PER_PAIR)
                sp.sem_inc(wvo_copied, -2)

        @block.scalar
        def _(act):
            for s in (*plain_stored, wvo_stored):
                act.sem_inc(s, 16)
            act.wait_ge(w_loaded, 16 * NW)
            act.sem_inc(w_loaded, -16 * NW)
            split_hi(0)
            with act.Fori(0, PAIRS // 2) as i:
                for j in range(2):
                    for c in range(NC):
                        for g in range(2):
                            act.wait_ge(plain_ready, PER_PAIR * j + 2 * c + g + 1)
                            act.wait_ge(plain_stored[g], 16)
                            act.sem_inc(plain_stored[g], -16)
                            nc.scalar.copy(plain_out[:, g, :], ps[:, PLAIN0 + g, :]).then_inc(plain_done, 1)
                        if c == 1:
                            act.wait_ge(w_loaded, 16 * NW * (j + 1))
                            split_hi(1 - j)
                            nc.scalar.copy(wo[0][:], wo_raw[:]).then_inc(wo_hi_ready, 1)
                        if c == NC - 1:
                            act.wait_ge(wv_turned, j + 1)
                            nc.scalar.copy(wvT[0][:], ps[:, WV_BANK, 0:2 * P].rearrange("p (h n) -> p h n", h=2)
                                           ).then_inc(wv_hi_ready, 1)
                    act.wait_ge(wvo_ready, j + 1)
                    act.wait_ge(wvo_stored, 16)
                    act.sem_inc(wvo_stored, -16)
                    nc.scalar.copy(wvo_out[:], ps[:, WVO0:WVO0 + 2, :]).then_inc(wvo_copied, 1)
                act.sem_inc(plain_ready, -2 * PER_PAIR)
                act.sem_inc(w_loaded, -2 * 16 * NW)
                act.sem_inc(wv_turned, -2)
                act.sem_inc(wvo_ready, -2)
            for s in (*plain_stored, wvo_stored):
                act.wait_ge(s, 16)

        @block.gpsimd
        def _(pool):
            for s in rot_stored:
                pool.sem_inc(s, 16)
            pool.wait_ge(w_hi_ready, 1)
            pool.sem_inc(w_hi_ready, -1)
            split_lo(0)
            with pool.Fori(0, PAIRS // 2) as i:
                for j in range(2):
                    for c in range(NC):
                        for g in range(2):
                            pool.wait_ge(multiplied, PER_PAIR * j + 2 * c + g + 1)
                            pool.wait_ge(rot_stored[g], 16)
                            pool.sem_inc(rot_stored[g], -16)
                            nc.gpsimd.tensor_tensor(rot_out[:, g, :], by_cos[:, g, :], by_sin[:, g, :],
                                                    ALU.add).then_inc(rot_done, 1)
                        if c == 1:
                            pool.wait_ge(w_hi_ready, j + 1)
                            split_lo(1 - j)
                pool.sem_inc(multiplied, -2 * PER_PAIR)
                pool.sem_inc(w_hi_ready, -2)
            for s in rot_stored:
                pool.wait_ge(s, 16)

        @block.vector
        def _(dve):
            dve.wait_ge(tables_loaded, 32)
            half = P // 2
            with dve.Fori(0, PAIRS // 2) as i:
                for j in range(2):
                    for c in range(NC):
                        toks = slice(c * CH, (c + 1) * CH)
                        for g in range(2):
                            dve.wait_ge(rot_ready, PER_PAIR * j + 2 * c + g + 1)
                            nc.vector.tensor_tensor(by_cos[:, g, :], ps[:, g, :], cos[:, toks], ALU.mult)
                            nc.vector.tensor_tensor(by_sin[0:half, g, :], ps[half:P, g, :],
                                                    sin[half:P, toks], ALU.mult)
                            nc.vector.tensor_tensor(by_sin[half:P, g, :], ps[0:half, g, :],
                                                    sin[0:half, toks], ALU.mult).then_inc(multiplied, 1)
                        if c == 2:
                            dve.wait_ge(wo_hi_ready, j + 1)
                            nc.vector.tensor_tensor(wo[1][:], wo_raw[:], wo[0][:].bitcast(F32), ALU.subtract)
                        if c == NC - 1:
                            dve.wait_ge(wv_hi_ready, j + 1)
                            nc.vector.tensor_tensor(wvT[1][:],
                                                    ps[:, WV_BANK, 0:2 * P].rearrange("p (h n) -> p h n", h=2),
                                                    wvT[0][:].bitcast(F32), ALU.subtract).then_inc(wv_lo_ready, 1)
                dve.sem_inc(rot_ready, -2 * PER_PAIR)
                dve.sem_inc(wv_hi_ready, -2)
                dve.sem_inc(wo_hi_ready, -2)

        @block.tensor
        def _(pe):
            pe.sem_inc(rot_bank_free, 2)
            pe.sem_inc(plain_bank_free, 2)
            with pe.Fori(0, PAIRS // 2) as i:
                for j in range(2):
                    pe.wait_ge(w_lo_ready, j + 1)

                    def product(bank, first, right, slices, toks):
                        n = 0
                        for k in range(slices):
                            for a, b in parts(0, 1):
                                mm = nc.tensor.matmul(ps[:, bank, :], w[j][a][:, first + k, :],
                                                      right[b][:, k, toks],
                                                      start=(n == 0), stop=(n == 3 * slices - 1))
                                n += 1
                        return mm

                    for c in range(NC):
                        toks = slice(c * CH, (c + 1) * CH)
                        for g in range(2):
                            n = PER_PAIR * j + 2 * c + g + 1
                            pe.wait_ge(rot_bank_free, n)
                            product(g, *ROT[g][1:2], ROT[g][2], ROT[g][3], toks).then_inc(rot_ready, 1)
                        if c == NC - 1:
                            pe.wait_ge(w_lo_ready, j + 2)
                            for h in range(2):
                                last = nc.tensor.transpose(ps[:, WV_BANK, h * P:(h + 1) * P],
                                                           wv_raw[:, h, :], ident[:, :])
                            last.then_inc(wv_turned, 1)
                        for g in range(2):
                            n = PER_PAIR * j + 2 * c + g + 1
                            pe.wait_ge(plain_bank_free, n)
                            product(PLAIN0 + g, *PLAIN[g][1:2], PLAIN[g][2], PLAIN[g][3],
                                    toks).then_inc(plain_ready, 1)
                    pe.wait_ge(wv_lo_ready, j + 1)
                    for h in range(2):
                        for n, (a, b) in enumerate(parts(0, 1)):
                            last = nc.tensor.matmul(ps[:, WVO0 + h, :], wvT[a][:, h, :], wo[b][:, h, :],
                                                    start=(n == 0), stop=(n == 2))
                    last.then_inc(wvo_ready, 1)
                pe.sem_inc(w_lo_ready, -2)
                pe.sem_inc(rot_bank_free, -2 * PER_PAIR)
                pe.sem_inc(plain_bank_free, -2 * PER_PAIR)
                pe.sem_inc(wv_lo_ready, -2)


QCH = 256
TPU = QCH // P
UPH = T // QCH
UNITS = 2 * UPH
PIECE = CH
RING = 4
SPLITS = 2 * NC + 1


def pieces(c):
    keys = (c + 1) * QCH
    return [(k, min(PIECE, keys - k)) for k in range(0, keys, PIECE)]


def attention_plan():
    steps = [(u, s) for u in range(UNITS) for s in range(u % UPH + 1)]
    first = [steps.index((u, 0)) for u in range(UNITS)]
    in_turn = {}
    for u in range(UNITS):
        n = u % UPH + 1
        for s in range(n):
            in_turn.setdefault(2 * u + 3 + (s >= (n + 1) // 2), []).append(first[u] + s)
    plan = []
    scored = softened = 0

    def soften(softmax, count):
        nonlocal softened
        for _ in range(min(count, len(softmax))):
            plan.append(softmax.pop(0))
            softened += 1

    for g in range(TPU * UNITS + 5):
        todo = in_turn.get(g, [])
        score, softmax, out = [], [], []
        if g < TPU * UNITS:
            u, t = divmod(g, TPU)
            score = [("scores", u, t, p) for p in range(len(pieces(u % UPH)))]
        if 0 < g <= TPU * UNITS:
            u, t = divmod(g - 1, TPU)
            softmax = [("exp", u, t, p) for p in range(len(pieces(u % UPH)))]
        if g >= 5:
            out = [("out", *divmod(g - 5, TPU))]
        at = []
        for p in range(len(score)):
            leaves = max(scored + p - RING + 1 - softened, 0)
            at.append(min(max(at[-1] + 1 if at else 0, leaves + 1 if leaves else 0), len(todo)))

        def score_next(k):
            nonlocal scored
            while score and at[0] <= k:
                soften(softmax, scored - RING + 1 - softened)
                plan.append(score.pop(0))
                at.pop(0)
                scored += 1

        if todo and todo[0] in first:
            score_next(0)
            plan.append(("turn", todo[0], *steps[todo[0]]))
            at = [max(x - 1, 0) for x in at]
        for k, n in enumerate(todo + [None]):
            if n is not None and n + 1 < len(steps) and n + 1 not in first:
                plan.append(("turn", n + 1, *steps[n + 1]))
            soften(softmax, 1)
            score_next(k)
            if n in first and out:
                plan.append(out.pop(0))
            if n is not None:
                plan.append(("values", n, *steps[n]))
            if out:
                plan.append(out.pop(0))
            if n is not None and (n + 1 == len(steps) or n + 1 in first):
                plan.append(("sums", steps[n][0]))
        soften(softmax, len(softmax))
        j, c = divmod(g // TPU, UPH)
        k = TPU * (c - 2) + g % TPU
        if j < 2 and 0 <= k < SPLITS:
            plan.append(("split", j, k))
    return plan


def attention(nc, hbm, keep):
    y, kv, ident = keep["y"], keep["kv"], keep["ident"]
    plan = attention_plan()
    tile_pieces = [(u, t, p) for u in range(UNITS) for t in range(TPU) for p in range(len(pieces(u % UPH)))]
    NPIECES = len(tile_pieces)
    NSTEPS = sum(e[0] == "values" for e in plan)
    piece_no = {x: n for n, x in enumerate(tile_pieces)}
    with ExitStack() as ctx:
        def sb(name, shape, dt=F32):
            return ctx.enter_context(nc.sbuf_tensor(name, shape, dt))

        def sem(name):
            return ctx.enter_context(nc.semaphore(name))

        k_raw, q_raw, w_raw = sb("k_raw", [P, T]), sb("q_raw", [P, T]), sb("wvo_raw", [P, D])
        k = [[sb(f"k_{n}{j}", [P, T], F32R) for n in ("hi", "lo")] for j in range(2)]
        q = [[sb(f"q_{n}{j}", [P, T], F32R) for n in ("hi", "lo")] for j in range(2)]
        w = [[sb(f"wvo_{n}{j}", [P, D], F32R) for n in ("hi", "lo")] for j in range(2)]
        probs = sb("probs", [P, 2, TPU, T])
        turned = [sb(f"turned_{n}", [P, 2, 2, QCH], F32R) for n in ("hi", "lo")]
        o = [sb(f"o_{n}", [P, 2, QCH], F32R) for n in ("hi", "lo")]
        negmax = sb("negmax", [P, 2, RING])
        bias = sb("bias", [P, 2, TPU])
        sums = sb("sums", [P, 4, TPU, RING])
        total = sb("total", [P, 2, TPU])
        share = sb("share", [P, 2, TPU])
        mask_raw = sb("mask_raw", [P, TPU, QCH])
        mask = sb("mask", [P, TPU, QCH], BF16)
        identb = sb("identb", [P, P], BF16)

        ps_scores = ctx.enter_context(nc.psum_tensor("ps_scores", [P, RING, PIECE], F32))
        ps_turn = ctx.enter_context(nc.psum_tensor("ps_turn", [P, 2, 2, QCH], F32))
        ps_o = ctx.enter_context(nc.psum_tensor("ps_o", [P, 2, D], F32))

        y_loaded = sem("y_loaded")
        mask_loaded = sem("mask_loaded")
        mask_ready = sem("mask_ready")
        k_loaded, q_loaded, w_loaded = sem("k_loaded"), sem("q_loaded"), sem("wvo_loaded")
        raw_free = sem("raw_free")
        split_hi_ready = sem("split_hi_ready")
        split_ready = sem("split_ready")
        scores_ready = sem("scores_ready")
        max_done = sem("max_done")
        bias_ready = sem("bias_ready")
        exp_done = sem("exp_done")
        turn_ready = sem("turn_ready")
        turned_hi_ready = sem("turned_hi_ready")
        turned_hi_told = sem("turned_hi_told")
        turned_lo_ready = sem("turned_lo_ready")
        o_ready = sem("o_ready")
        o_hi_ready = sem("o_hi_ready")
        o_lo_ready = sem("o_lo_ready")
        out_ready = sem("out_ready")
        share_done = sem("share_done")
        out_added = sem("out_added")

        def bias_of(u, t):
            return bias[:, u % 2, t:t + 1]

        def load_head(sp, pair, head):
            pr = bass.ds(pair, 1)
            for n, raw, done in ((1, k_raw, k_loaded), (0, q_raw, q_loaded)):
                sp.dma_start(raw[0:ND, :], hbm["plainT"][n, pr, ND * head:ND * (head + 1), :]).then_inc(done, 16)
                for f in range(2):
                    r = P // 2 * f + HALF * head
                    sp.dma_start(raw[ND + HALF * f:ND + HALF * (f + 1), :],
                                 hbm["rotT"][n, pr, r:r + HALF, :]).then_inc(done, 16)
            sp.dma_start(w_raw[:], hbm["wvo"].rearrange("(q h p) n -> q h p n", h=2, p=P)[pr, head, :, :]
                         ).then_inc(w_loaded, 16)

        def split_views(j, n):
            if n == 2 * NC:
                return w_raw[:], w[j][0][:], w[j][1][:]
            raw, (hi, lo) = (q_raw, q[j]) if n % 2 else (k_raw, k[j])
            cols = slice(n // 2 * CH, (n // 2 + 1) * CH)
            return raw[:, cols], hi[:, cols], lo[:, cols]

        def split_hi(act, j, n, heads_before):
            if n in (0, 1, 2 * NC):
                loaded, loads = {0: (k_loaded, 3), 1: (q_loaded, 3), 2 * NC: (w_loaded, 1)}[n]
                act.wait_ge(loaded, 16 * loads * (heads_before + 1))
            raw, hi, _ = split_views(j, n)
            nc.scalar.copy(hi, raw).then_inc(split_hi_ready, 1)

        def split_lo(pool, j, n, before):
            pool.wait_ge(split_hi_ready, before + n + 1)
            raw, hi, lo = split_views(j, n)
            nc.gpsimd.tensor_tensor(lo, raw, hi.bitcast(F32), ALU.subtract).then_inc(split_ready, 1)

        block = ctx.enter_context(nc.Block())

        @block.sync
        def _(sp):
            sp.dma_start(mask_raw[:], hbm["mask"]).then_inc(mask_loaded, 16)
            load_head(sp, 0, 0)
            for m in range(4):
                sp.dma_start(y[:, 4 * m:4 * m + 4, :],
                             hbm["x"].rearrange("(t p) d -> p t d", p=P)[:, 4 * m:4 * m + 4, :]
                             ).then_inc(y_loaded, 16)
            with sp.Fori(0, PAIRS) as i:
                for j in range(2):
                    sp.wait_ge(raw_free, j + 1)
                    load_head(sp, i if j == 0 else sp.snap((i + 1) % PAIRS), 1 - j)
                sp.sem_inc(raw_free, -2)

        @block.gpsimd
        def _(pool):
            for n in range(SPLITS):
                split_lo(pool, 0, n, 0)
            pool.sem_inc(split_hi_ready, -SPLITS)
            pool.drain().then_inc(raw_free, 1)
            with pool.Fori(0, PAIRS) as i:
                for j in range(2):
                    for n in range(SPLITS):
                        split_lo(pool, 1 - j, n, SPLITS * j)
                    pool.drain().then_inc(raw_free, 1)
                pool.sem_inc(split_hi_ready, -2 * SPLITS)

        @block.scalar
        def _(act):
            act.wait_ge(mask_loaded, 16)
            nc.scalar.copy(mask[:], mask_raw[:])
            nc.scalar.copy(identb[:], ident[:]).then_inc(mask_ready, 1)
            for n in range(SPLITS):
                split_hi(act, 0, n, 0)
            act.sem_inc(k_loaded, -48)
            act.sem_inc(q_loaded, -48)
            act.sem_inc(w_loaded, -16)
            with act.Fori(0, PAIRS) as i:
                for kind, *args in plan:
                    if kind == "split":
                        j, n = args
                        split_hi(act, 1 - j, n, j)
                    if kind == "exp":
                        u, t, p = args
                        n = piece_no[u, t, p]
                        first_key, keys = pieces(u % UPH)[p]
                        act.wait_ge(bias_ready, TPU * u + t + 1)
                        nc.scalar.activation(probs[:, u % 2, t, first_key:first_key + keys],
                                             ps_scores[:, n % RING, 0:keys], ACT.Exp,
                                             bias=bias_of(u, t),
                                             accum_out=sums[:, u % 4, t, p:p + 1]).then_inc(exp_done, 1)
                    if kind == "turn":
                        n, u, s = args
                        act.wait_ge(turn_ready, n + 1)
                        nc.scalar.copy(turned[0][:, n % 2], ps_turn[:, n % 2]).then_inc(turned_hi_ready, 1)
                    if kind == "sums":
                        u, = args
                        act.wait_ge(o_ready, u + 1)
                        nc.scalar.copy(o[0][:, u % 2, :], ps_o[:, u % 2, 0:QCH]).then_inc(o_hi_ready, 1)
                act.sem_inc(k_loaded, -96)
                act.sem_inc(q_loaded, -96)
                act.sem_inc(w_loaded, -32)
                act.sem_inc(bias_ready, -TPU * UNITS)
                act.sem_inc(turn_ready, -NSTEPS)
                act.sem_inc(o_ready, -UNITS)

        @block.vector
        def _(dve):
            dve.wait_ge(y_loaded, 64)
            with dve.Fori(0, PAIRS) as i:
                maxima = 0
                for kind, *args in plan:
                    if kind == "scores":
                        u, t, p = args
                        tile = pieces(u % UPH)
                        n = piece_no[u, t, p]
                        dve.wait_ge(scores_ready, n + 1)
                        whole = len(tile) == 1
                        put = bias_of(u, t) if whole else negmax[:, t, p:p + 1]
                        nc.vector.tensor_reduce(put, ps_scores[:, n % RING, 0:tile[p][1]], AX_X, ALU.max,
                                                negate=True).then_inc(bias_ready if whole else max_done, 1)
                        if p + 1 == len(tile) and not whole:
                            maxima += len(tile)
                            dve.wait_ge(max_done, maxima)
                            nc.vector.tensor_reduce(bias_of(u, t), negmax[:, t, 0:len(tile)], AX_X, ALU.min
                                                    ).then_inc(bias_ready, 1)
                    if kind == "turn":
                        n, u, s = args
                        dve.wait_ge(turned_hi_ready, n + 1)
                        dve.sem_inc(turned_hi_told, 1)
                        nc.vector.tensor_tensor(turned[1][:, n % 2], ps_turn[:, n % 2],
                                                turned[0][:, n % 2].bitcast(F32),
                                                ALU.subtract).then_inc(turned_lo_ready, 1)
                    if kind == "sums":
                        u, = args
                        dve.wait_ge(o_hi_ready, u + 1)
                        nc.vector.tensor_tensor(o[1][:, u % 2, :], ps_o[:, u % 2, 0:QCH],
                                                o[0][:, u % 2, :].bitcast(F32), ALU.subtract).then_inc(o_lo_ready, 1)
                    if kind == "out":
                        u, t = args
                        dve.wait_ge(out_ready, TPU * u + t + 1)
                        if t == 0:
                            nc.vector.tensor_reduce(total[:, u % 2, :], sums[:, u % 4, :, 0:len(pieces(u % UPH))],
                                                    AX_X, ALU.add).then_inc(share_done, 1)
                            dve.wait_ge(share_done, 2 * u + 1)
                            nc.vector.reciprocal(share[:, u % 2, :], total[:, u % 2, :]).then_inc(share_done, 1)
                            dve.wait_ge(share_done, 2 * u + 2)
                        row = TPU * (u % UPH) + t
                        nc.vector.scalar_tensor_tensor(y[:, row, :], ps_o[:, u % 2, :], share[:, u % 2, t:t + 1], y[:, row, :],
                                                       ALU.mult, ALU.add).then_inc(out_added, 1)
                dve.sem_inc(scores_ready, -NPIECES)
                dve.sem_inc(max_done, -maxima)
                dve.sem_inc(turned_hi_ready, -NSTEPS)
                dve.sem_inc(o_hi_ready, -UNITS)
                dve.sem_inc(out_ready, -TPU * UNITS)
                dve.sem_inc(share_done, -2 * UNITS)

        @block.tensor
        def _(pe):
            pe.wait_ge(mask_ready, 1)
            pe.sem_inc(exp_done, RING)
            pe.sem_inc(turned_lo_ready, 2)
            pe.sem_inc(out_added, 1)
            with pe.Fori(0, PAIRS) as i:
                for kind, *args in plan:
                    if kind == "scores":
                        u, t, p = args
                        j, c = divmod(u, UPH)
                        n = piece_no[u, t, p]
                        first_key, keys = pieces(c)[p]
                        row = TPU * c + t
                        if c % 2 == 0 and (t, p) == (0, 0):
                            pe.wait_ge(split_ready, SPLITS * j + c + 2)
                        pe.wait_ge(exp_done, n + 1)
                        diagonal = first_key + keys == (c + 1) * QCH
                        for m, (x, z) in enumerate(parts(0, 1)):
                            last = nc.tensor.matmul(ps_scores[:, n % RING, 0:keys], q[j][x][:, row * P:(row + 1) * P],
                                                    k[j][z][:, first_key:first_key + keys],
                                                    start=(m == 0), stop=(m == 2 and not diagonal))
                        if diagonal:
                            last = nc.tensor.matmul(ps_scores[:, n % RING, keys - QCH:keys], identb[:], mask[:, t, :],
                                                    start=False, stop=True)
                        last.then_inc(scores_ready, 1)
                    if kind == "turn":
                        n, u, s = args
                        if s == 0:
                            pe.wait_ge(exp_done, RING + piece_no[u, TPU - 1, len(pieces(u % UPH)) - 1] + 1)
                        pe.wait_ge(turned_lo_ready, n + 1)
                        for kb in range(2):
                            for t in range(TPU):
                                key = (2 * s + kb) * P
                                last = nc.tensor.transpose(ps_turn[:, n % 2, kb, t * P:(t + 1) * P],
                                                           probs[:, u % 2, t, key:key + P], ident[:])
                        last.then_inc(turn_ready, 1)
                    if kind == "values":
                        n, u, s = args
                        if s == 0:
                            pe.wait_ge(out_added, 1 + max(TPU * (u - 1), 0))
                        products = [(x, z, kb) for x, z in ((0, 0), (1, 0), (0, 1)) for kb in range(2)]
                        for m, (x, z, kb) in enumerate(products):
                            if m == 0:
                                pe.wait_ge(turned_hi_told, n + 1)
                            if z and kb == 0:
                                pe.wait_ge(turned_lo_ready, 2 + n + 1)
                            last = nc.tensor.matmul(ps_o[:, u % 2, 0:QCH], kv[x][:, 2 * s + kb, :],
                                                    turned[z][:, n % 2, kb, :],
                                                    start=(s == 0 and m == 0),
                                                    stop=(s == u % UPH and m == len(products) - 1))
                        if s == u % UPH:
                            last.then_inc(o_ready, 1)
                    if kind == "out":
                        u, t = args
                        if t == 0 and u % UPH == 0:
                            pe.wait_ge(split_ready, SPLITS * (u // UPH + 1))
                        if t == 0:
                            pe.wait_ge(o_lo_ready, u + 1)
                        pe.wait_ge(out_added, TPU * u + t + 1)
                        for m, (x, z) in enumerate(parts(0, 1)):
                            last = nc.tensor.matmul(ps_o[:, u % 2, :], o[x][:, u % 2, t * P:(t + 1) * P], w[u // UPH][z][:],
                                                    start=(m == 0), stop=(m == 2))
                        last.then_inc(out_ready, 1)
                pe.sem_inc(split_ready, -2 * SPLITS)
                pe.sem_inc(exp_done, -NPIECES)
                pe.sem_inc(turned_hi_told, -NSTEPS)
                pe.sem_inc(turned_lo_ready, -NSTEPS)
                pe.sem_inc(o_lo_ready, -UNITS)
                pe.sem_inc(out_added, -TPU * UNITS)


ET = E // P
QUARTERS = 4


def ternary_weights(nc, hbm, keep, ffn):
    y, ident = keep["y"], keep["ident"]
    wT, scale, mv, rstd = ffn["wT"], ffn["scale"], ffn["mv"], ffn["rstd"]
    QW = D * E // P // QUARTERS
    sources = (hbm["W_up"].rearrange("(r p) n -> p r n", p=P),
               hbm["W_gate"].rearrange("(r p) n -> p r n", p=P),
               hbm["W_down"].rearrange("(r p) n -> p r n", p=P))
    with ExitStack() as ctx:
        def sb(name, shape, dt=F32):
            return ctx.enter_context(nc.sbuf_tensor(name, shape, dt))

        def sem(name):
            return ctx.enter_context(nc.semaphore(name))

        raw = [sb(f"ternary_raw{m}", [P, QUARTERS, QW]) for m in range(2)]
        signs = sb("signs", [P, 2, QW], BF16)
        abs_sums = sb("abs_sums", [P, 3, QUARTERS])
        total = sb("abs_total", [P, 3])
        bound = sb("bound", [P, 3, 2])
        ones = sb("ones", [P, P])
        identb = sb("identb3", [P, P], BF16)
        bn = sb("bn3", [P, 2, 6])
        std = sb("std3", [P, NT])
        ps_turn = ctx.enter_context(nc.psum_tensor("ps_signs", [P, 4, 2 * CH], BF16))
        ps_sum = ctx.enter_context(nc.psum_tensor("ps_abs", [P, CH], F32))

        loaded = [[sem(f"ternary_loaded{b}{q}") for q in range(QUARTERS)] for b in range(2)]
        ones_ready = sem("ones_ready")
        identb_ready = sem("identb_ready")
        stats_done = sem("stats3_done")
        var_ready = sem("var3_ready")
        std_ready = sem("std3_ready")
        abs_ready = sem("abs_ready")
        abs_summed = sem("abs_summed")
        scale_done = sem("scale_done")
        below_done = sem("below_done")
        signs_ready = sem("signs_ready")
        signs_turned = sem("signs_turned")
        signs_copied = sem("signs_copied")
        signs_free = sem("signs_free")
        raw_free = sem("ternary_raw_free")

        block = ctx.enter_context(nc.Block())

        @block.sync
        def _(sp):
            for m in range(3):
                for q in range(QUARTERS):
                    if m == 2:
                        sp.wait_ge(raw_free, q + 1)
                    n = (ET if m < 2 else KD) // QUARTERS
                    sp.dma_start(raw[m % 2][:, q, :].rearrange("p (r n) -> p r n", r=n),
                                 sources[m][:, n * q:n * (q + 1), :]).then_inc(loaded[m % 2][q], 16)

        @block.gpsimd
        def _(pool):
            nc.gpsimd.memset(ones[:], 1.0).then_inc(ones_ready, 1)

        @block.scalar
        def _(act):
            nc.scalar.copy(identb[:], ident[:]).then_inc(identb_ready, 1)
            act.wait_ge(var_ready, 1)
            nc.scalar.activation(std[:], std[:], ACT.Sqrt).then_inc(std_ready, 1)

            def abs_sum(m, q):
                act.wait_ge(loaded[m % 2][q], 16 * (m // 2 + 1))
                unused = (wT[1][:, q, :] if m == 1 else
                          wT[2][:, QW // D * q:QW // D * (q + 1), :].rearrange("p r n -> p (r n)"))
                nc.scalar.activation(unused, raw[m % 2][:, q, :], ACT.Abs,
                                     accum_out=abs_sums[:, m, q:q + 1]).then_inc(abs_ready, 1)

            for q in range(QUARTERS):
                abs_sum(0, q)
            for m in range(3):
                for q in range(QUARTERS):
                    if m < 2:
                        abs_sum(m + 1, q)
                    for b in range(4):
                        act.wait_ge(signs_turned, 16 * m + 4 * q + b + 1)
                        turned = ps_turn[:, b, 0:CH]
                        if m < 2:
                            put = wT[m][:, b, q * CH:(q + 1) * CH]
                        else:
                            put = wT[m][:, 4 * b:4 * b + 4, q * P:(q + 1) * P]
                            turned = turned.rearrange("p (e n) -> p e n", e=4)
                        nc.scalar.copy(put, turned).then_inc(signs_copied, 1)
                    act.sem_inc(signs_free, 1)
                    if m == 0:
                        act.sem_inc(raw_free, 1)

        @block.vector
        def _(dve):
            for t in range(NT):
                nc.vector.bn_stats(bn[:, t % 2, :], y[:, t, :]).then_inc(stats_done, 1)
                dve.wait_ge(stats_done, 2 * t + 1)
                nc.vector.bn_aggr(mv[:, t, :], bn[:, t % 2, :]).then_inc(stats_done, 1)
            dve.wait_ge(stats_done, 2 * NT)
            nc.vector.tensor_scalar(std[:], mv[:, :, 1], LN_EPS, None, ALU.add).then_inc(var_ready, 1)
            dve.wait_ge(std_ready, 1)
            nc.vector.reciprocal(rstd[:], std[:])
            for m in range(3):
                dve.wait_ge(abs_summed, m + 1)
                nc.vector.tensor_reduce(total[:, m:m + 1], ps_sum[:, 4 * m:4 * m + 4], AX_X, ALU.add
                                        ).then_inc(scale_done, 1)
                dve.wait_ge(scale_done, 3 * m + 1)
                nc.vector.tensor_scalar(scale[:, m:m + 1], total[:, m:m + 1], 1.0 / (D * E), QUANT_EPS,
                                        ALU.mult, ALU.add).then_inc(scale_done, 1)
                dve.wait_ge(scale_done, 3 * m + 2)
                nc.vector.tensor_scalar(bound[:, m, 0:1], scale[:, m:m + 1], 0.5, None, ALU.mult)
                nc.vector.tensor_scalar(bound[:, m, 1:2], scale[:, m:m + 1], -0.5, None, ALU.mult
                                        ).then_inc(scale_done, 1)
                dve.wait_ge(scale_done, 3 * m + 3)
                for q in range(QUARTERS):
                    n = QUARTERS * m + q
                    if n >= 2:
                        dve.wait_ge(signs_free, n - 1)
                    below = signs[:, n % 2, :]
                    nc.vector.tensor_scalar(below, raw[m % 2][:, q, :], bound[:, m, 1:2], None,
                                            ALU.is_lt).then_inc(below_done, 1)
                    dve.wait_ge(below_done, n + 1)
                    nc.vector.scalar_tensor_tensor(signs[:, n % 2, :], raw[m % 2][:, q, :], bound[:, m, 0:1], below,
                                                   ALU.is_gt, ALU.subtract).then_inc(signs_ready, 1)

        @block.tensor
        def _(pe):
            pe.wait_ge(ones_ready, 1)
            pe.wait_ge(identb_ready, 1)
            for m in range(3):
                pe.wait_ge(abs_ready, QUARTERS * (m + 1))
                nc.tensor.matmul(ps_sum[:, 4 * m:4 * m + 4], ones[:], abs_sums[:, m, :],
                                 start=True, stop=True).then_inc(abs_summed, 1)
                for q in range(QUARTERS):
                    n = QUARTERS * m + q
                    pe.wait_ge(signs_ready, n + 1)
                    for b in range(4):
                        if n:
                            pe.wait_ge(signs_copied, 4 * (n - 1) + b + 1)
                        for r in range(4):
                            at = (r * D + b * P) if m < 2 else (4 * b + r) * P
                            last = nc.tensor.transpose(ps_turn[:, b, r * P:(r + 1) * P],
                                                       signs[:, n % 2, at:at + P], identb[:])
                        last.then_inc(signs_turned, 1)


def feed_forward(nc, hbm, keep, ffn, out):
    y, ident = keep["y"], keep["ident"]
    wT, scale, mv, rstd = ffn["wT"], ffn["scale"], ffn["mv"], ffn["rstd"]
    UP, GATE, DOWN = range(3)
    NORM_AT = {2 + 3 * t: t for t in range(TC)}
    with ExitStack() as ctx:
        def sb(name, shape, dt=F32):
            return ctx.enter_context(nc.sbuf_tensor(name, shape, dt))

        def sem(name):
            return ctx.enter_context(nc.semaphore(name))

        xn = sb("xn3", [P, 2, D])
        hT = [sb(f"hT_{n}", [P, 2, KD, CH], F32R) for n in ("hi", "lo")]
        gated = sb("gated", [P, CH])
        hidden = sb("hidden", [P, CH])
        hid = [sb(f"hidden_{n}", [P, 2, CH], F32R) for n in ("hi", "lo")]
        result = sb("result", [P, TC, D])
        ps_acc = ctx.enter_context(nc.psum_tensor("ps_acc", [P, TC, D], F32))
        ps_up = ctx.enter_context(nc.psum_tensor("ps_up", [P, 2, CH], F32))
        ps_gate = ctx.enter_context(nc.psum_tensor("ps_gate", [P, CH], F32))
        ps_turn = ctx.enter_context(nc.psum_tensor("ps_turn3", [P, D], F32))

        xn_ready = sem("xn3_ready")
        turn_ready = sem("turn3_ready")
        h_hi_ready = sem("h_hi_ready")
        h_lo_ready = sem("h_lo_ready")
        up_ready = sem("up_ready")
        silu_ready = sem("silu_ready")
        gate_ready = sem("gate_ready")
        hidden_ready = sem("hidden_ready")
        hid_hi_ready = sem("hid_hi_ready")
        hid_lo_ready = sem("hid_lo_ready")
        acc_ready = sem("acc_ready")
        result_ready = sem("result_ready")
        acc_free = sem("acc_free")
        stored = [sem(f"stored{t}") for t in range(TC)]

        block = ctx.enter_context(nc.Block())

        def h_tile(part, slot, t):
            return hT[part][:, bass.ds(slot, 1), :, t * P:(t + 1) * P]

        def turned():
            return ps_turn[:].rearrange("p (k n) -> p k n", k=KD)

        @block.vector
        def _(dve):
            def normalise(chunk, t):
                row = bass.ds(chunk * TC + t, 1)
                nc.vector.tensor_scalar(xn[:, t % 2, :], y[:, row, :], mv[:, row, 0], rstd[:, row],
                                        ALU.subtract, ALU.mult).then_inc(xn_ready, 1)

            def h_low(slot, t, count):
                dve.wait_ge(h_hi_ready, count)
                nc.vector.tensor_tensor(h_tile(1, slot, t), turned(), h_tile(0, slot, t).bitcast(F32),
                                        ALU.subtract).then_inc(h_lo_ready, 1)

            for t in range(TC):
                normalise(0, t)
                h_low(0, t, t + 1)
            dve.sem_inc(h_hi_ready, -TC)
            for s in stored:
                dve.sem_inc(s, 16)
            with dve.Fori(0, NC) as i:
                following, slot = dve.snap((i + 1) % NC), dve.snap((i + 1) % 2)
                for e in range(ET):
                    if e in NORM_AT:
                        normalise(following, NORM_AT[e])
                    dve.wait_ge(silu_ready, e + 1)
                    dve.wait_ge(gate_ready, e + 1)
                    nc.vector.scalar_tensor_tensor(hidden[:], ps_gate[:], scale[:, GATE:GATE + 1], gated[:],
                                                   ALU.mult, ALU.mult).then_inc(hidden_ready, 1)
                    dve.wait_ge(hid_hi_ready, e + 1)
                    nc.vector.tensor_tensor(hid[1][:, e % 2, :], hidden[:], hid[0][:, e % 2, :].bitcast(F32),
                                            ALU.subtract).then_inc(hid_lo_ready, 1)
                    if e in NORM_AT:
                        h_low(slot, NORM_AT[e], NORM_AT[e] + 1)
                for t in range(TC):
                    dve.wait_ge(acc_ready, t + 1)
                    dve.wait_ge(stored[t], 16)
                    dve.sem_inc(stored[t], -16)
                    nc.vector.scalar_tensor_tensor(result[:, t, :], ps_acc[:, t, :], scale[:, DOWN:DOWN + 1],
                                                   y[:, bass.ds(i * TC + t, 1), :].rearrange("p a n -> p (a n)"),
                                                   ALU.mult, ALU.add).then_inc(result_ready, 1)
                dve.sem_inc(silu_ready, -ET)
                dve.sem_inc(gate_ready, -ET)
                dve.sem_inc(hid_hi_ready, -ET)
                dve.sem_inc(h_hi_ready, -TC)
                dve.sem_inc(acc_ready, -TC)
            for s in stored:
                dve.wait_ge(s, 16)

        @block.sync
        def _(sp):
            with sp.Fori(0, NC) as i:
                for t in range(TC):
                    sp.wait_ge(result_ready, t + 1)
                    sp.sem_inc(acc_free, 1)
                    sp.dma_start(out.rearrange("(t p) d -> t p d", p=P)[bass.ds(i * TC + t, 1), :, :],
                                 result[:, t, :]).then_inc(stored[t], 16)
                sp.sem_inc(result_ready, -TC)

        @block.scalar
        def _(act):
            def h_high(slot, t, count):
                act.wait_ge(turn_ready, count)
                nc.scalar.copy(h_tile(0, slot, t), turned()).then_inc(h_hi_ready, 1)

            for t in range(TC):
                h_high(0, t, t + 1)
            act.sem_inc(turn_ready, -TC)
            with act.Fori(0, NC) as i:
                slot = act.snap((i + 1) % 2)
                for e in range(ET):
                    act.wait_ge(up_ready, e + 1)
                    nc.scalar.activation(gated[:], ps_up[:, e % 2, :], ACT.Silu, scale=scale[:, UP:UP + 1]
                                         ).then_inc(silu_ready, 1)
                    act.wait_ge(hidden_ready, e + 1)
                    nc.scalar.copy(hid[0][:, e % 2, :], hidden[:]).then_inc(hid_hi_ready, 1)
                    if e in NORM_AT:
                        h_high(slot, NORM_AT[e], NORM_AT[e] + 1)
                act.sem_inc(up_ready, -ET)
                act.sem_inc(hidden_ready, -ET)
                act.sem_inc(turn_ready, -TC)

        @block.tensor
        def _(pe):
            def turn(t):
                pe.wait_ge(xn_ready, t + 1)
                for k in range(KD):
                    last = nc.tensor.transpose(ps_turn[:, k * P:(k + 1) * P],
                                               xn[:, t % 2, k * P:(k + 1) * P], ident[:])
                last.then_inc(turn_ready, 1)

            def down(e):
                pe.wait_ge(hid_lo_ready, e + 1)
                for t in range(TC):
                    if e == 0:
                        pe.wait_ge(acc_free, t + 1)
                    for part in range(2):
                        last = nc.tensor.matmul(ps_acc[:, t, :], hid[part][:, e % 2, t * P:(t + 1) * P],
                                                wT[DOWN][:, e, :], start=(e == 0 and part == 0),
                                                stop=(e == ET - 1 and part == 1))
                    if e == ET - 1:
                        last.then_inc(acc_ready, 1)

            for t in range(TC):
                turn(t)
            pe.sem_inc(xn_ready, -TC)
            pe.sem_inc(acc_free, TC)
            with pe.Fori(0, NC) as i:
                slot = pe.snap(i % 2)
                pe.wait_ge(h_lo_ready, TC)
                for e in range(ET):
                    for m, bank, ready in ((UP, ps_up[:, e % 2, :], up_ready), (GATE, ps_gate[:], gate_ready)):
                        before = e - 1 if m == UP else e
                        if before > 0:
                            pe.wait_ge(hid_lo_ready, before)
                        for kk in range(KD):
                            for part in range(2):
                                last = nc.tensor.matmul(bank, wT[m][:, kk, e * P:(e + 1) * P],
                                                        hT[part][:, bass.ds(slot, 1), kk, :],
                                                        start=(kk == 0 and part == 0),
                                                        stop=(kk == KD - 1 and part == 1))
                        last.then_inc(ready, 1)
                    if e:
                        down(e - 1)
                    if e in NORM_AT:
                        turn(NORM_AT[e])
                down(ET - 1)
                pe.sem_inc(h_lo_ready, -TC)
                pe.sem_inc(hid_lo_ready, -ET)
                pe.sem_inc(acc_free, -TC)
                pe.sem_inc(xn_ready, -TC)


def program(nc, hbm, out):
    hbm["plainT"] = nc.dram_tensor("plainT", [2, PAIRS, P, T], F32, kind="Internal").ap()
    hbm["rotT"] = nc.dram_tensor("rotT", [2, PAIRS, P, T], F32, kind="Internal").ap()
    hbm["wvo"] = nc.dram_tensor("wvo", [H * P, D], F32, kind="Internal").ap()

    def sb(owner, name, shape, dt=F32):
        return owner.enter_context(nc.sbuf_tensor(name, shape, dt))

    def two(owner, name, shape):
        return [sb(owner, f"{name}_{n}", shape, F32R) for n in ("hi", "lo")]

    with ExitStack() as ctx:
        keep = {"ident": sb(ctx, "ident", [P, P])}
        place = nc.sbuf_base
        keep["y"] = sb(ctx, "y", [P, NT, D])
        qlatT = [nc.alloc_sbuf_tensor_at(f"qlatT_{n}", [P, KQ, T], F32R, offset=place + i * KQ * T * 4)
                 for i, n in enumerate(("hi", "lo"))]
        with ExitStack() as c1:
            keep["kv"] = two(c1, "kv", [P, NT, KVR])
            with ExitStack() as c2:
                xT, kvT = two(c2, "xT", [P, KD, T]), two(c2, "kvT", [P, T])
                latents(nc, hbm, keep, xT, qlatT, kvT)
                heads_inputs(nc, hbm, keep, xT, qlatT, kvT)
            attention(nc, hbm, keep)
        ffn = {"wT": [sb(ctx, f"wT_{n}", shape, F32R) for n, shape in
                      (("up", [P, KD, E]), ("gate", [P, KD, E]), ("down", [P, ET, D]))],
               "scale": sb(ctx, "scale", [P, 3]), "mv": sb(ctx, "mv3", [P, NT, 2]), "rstd": sb(ctx, "rstd3", [P, NT])}
        ternary_weights(nc, hbm, keep, ffn)
        feed_forward(nc, hbm, keep, ffn, out)


def constants():
    freq = (np.float32(1.0) / np.power(np.float32(ROPE_BASE), np.arange(HALF, dtype=np.float32) / np.float32(HALF)))
    angle = (np.arange(T, dtype=np.float32)[:, None] * freq.astype(np.float32)).T
    cos = np.tile(np.cos(angle).astype(np.float32), (4, 1))
    sin = np.tile(np.sin(angle).astype(np.float32), (4, 1))
    sin[P // 2:] *= np.float32(-1.0)
    query = np.arange(QCH).reshape(TPU, P).T[:, :, None]
    mask = np.where(np.arange(QCH)[None, None, :] > query, np.float32(NEG), np.float32(0.0)).astype(np.float32)
    return {"ident": np.eye(P, dtype=np.float32), "mask": mask, "cos": cos, "sin": sin}


NAMES = ("x", "Wq_down", "Wq_up", "Wq_rope", "Wkv_down", "Wk_up", "Wk_rope", "Wv_up", "Wo", "W_up", "W_gate", "W_down")


def kernel(**inputs):
    import concourse.bacc as bacc
    from concourse.bass_utils import run_bass_kernel_spmd

    nc = bacc.Bacc("TRN2", target_bir_lowering=False, num_devices=1)
    arrays = {}
    for name in NAMES:
        a = np.ascontiguousarray(inputs[f"L0_{'ffn' if name in ('W_up', 'W_gate', 'W_down') else 'attn'}_{name}"])
        arrays[name] = a.reshape(T, D) if name == "x" else a
    arrays.update(constants())
    hbm = {n: nc.dram_tensor(f"in_{n}", a.shape, mybir.dt.from_np(a.dtype), kind="ExternalInput").ap()
           for n, a in arrays.items()}
    out = nc.dram_tensor("out", [T, D], F32, kind="ExternalOutput").ap()
    program(nc, hbm, out)
    r = run_bass_kernel_spmd(nc, [{f"in_{n}": a for n, a in arrays.items()}], core_ids=[0])
    return r.results[0]["out"].reshape(1, T, D)
```

```python
from contextlib import ExitStack

import numpy as np

import concourse.bass as bass
from concourse import mybir

ALU = mybir.AluOpType
ACT = mybir.ActivationFunctionType
AX_X = mybir.AxisListType.X
F32 = mybir.dt.float32
F32R = mybir.dt.float32r
BF16 = mybir.dt.bfloat16

P = 128
LN_EPS = 1e-5
QUANT_EPS = 1e-8
NEG = -1e30
ROPE_BASE = 10000.0

T, D = 2048, 512
H, HD, RD = 16, 128, 64
HALF = RD // 2
ND = HD - RD
QR, KVR = 256, 128
E = 2048
ET = E // P
KD = D // P
KQ = QR // P
NT = T // P
CH = 512
NC = T // CH
TC = CH // P
PAIRS = H // 2
SCALE = float(HD) ** -0.5


MATS = ("W_up", "W_gate", "W_down")
WCH = D * E // P // PAIRS


def weight_chunks(w):
    return w.rearrange("a b -> (a b)").rearrange("(c p n) -> c p n", p=P, n=WCH)


def parts(hi, lo):
    return ((hi, hi), (hi, lo), (lo, hi))


ROT_Q, ROT_K, PLAIN_Q, PLAIN_K = 0, KQ, KQ + KD, 2 * KQ + KD
NSL = 2 * KQ + KD + 1
PAIR_LOADS = 4


def load_pair_weights(sp, hbm, pair_w, pair, loaded):
    cols = bass.ds(pair * P, P)
    for name, s0, k in (("Wq_rope", ROT_Q, KQ), ("Wk_rope", ROT_K, KD), ("Wq_up", PLAIN_Q, KQ), ("Wk_up", PLAIN_K, 1)):
        sp.dma_start(pair_w["raw"][:, s0:s0 + k, :],
                     hbm[name].rearrange("(k p) n -> p k n", p=P)[:, :, cols]).then_inc(loaded, 16)


def pair_views(pair_w, j):
    raw, (hi, lo) = pair_w["raw"], pair_w["split"][j]
    views = []
    for f in range(2):
        put = [z[:, 0:PLAIN_Q, :].rearrange("p k (f h r) -> p k f h r", h=2, f=2)[:, :, f] for z in (hi, lo)]
        views.append((raw[:, 0:PLAIN_Q, :].rearrange("p k (h f r) -> p k f h r", h=2, f=2)[:, :, f], *put))
    views.append(tuple(z[:, PLAIN_Q:NSL, :] for z in (raw, hi, lo)))
    return views


def latents(nc, hbm, keep, pair_w, xT, qlatT, kvT):
    ident, kv = keep["ident"], keep["kv"]
    NL = KQ + 1
    LAT0, KV0 = 2, 5
    AHEAD = 2
    SPLIT_AT = 1
    with ExitStack() as ctx:
        def sb(name, shape, dt=F32):
            return ctx.enter_context(nc.sbuf_tensor(name, shape, dt))

        def sem(name):
            return ctx.enter_context(nc.semaphore(name))

        x = sb("x", [P, NT, D])
        w_raw = sb("wlat_raw", [P, KD, QR + KVR])
        w = [sb(f"wlat_{n}", [P, KD, QR + KVR], F32R) for n in ("hi", "lo")]
        bn = sb("bn", [P, TC, 6])
        mv = sb("mv", [P, NT, 2])
        std = sb("std", [P, NT])
        rstd = sb("rstd", [P, NT])
        ps = ctx.enter_context(nc.psum_tensor("ps_lat", [P, 8, CH], F32))

        ident_loaded = sem("ident_loaded")
        x_loaded = [sem(f"x_loaded{i}") for i in range(NC)]
        wlat_loaded = sem("wlat_loaded")
        pair_loaded = sem("pair_loaded")
        stats_done = sem("stats_done")
        var_ready = sem("var_ready")
        std_ready = sem("std_ready")
        rstd_done = sem("rstd_done")
        rstd_ready = sem("rstd_ready")
        xn_ready = sem("xn_ready")
        xt_ready = sem("xt_ready")
        xt_hi_ready = sem("xt_hi_ready")
        xt_lo_ready = sem("xt_lo_ready")
        wlat_hi_ready = sem("wlat_hi_ready")
        wlat_lo_ready = sem("wlat_lo_ready")
        pair_hi_ready = sem("pair_hi_ready")
        lat_ready = sem("lat_ready")
        lat_hi_ready = sem("lat_hi_ready")
        lat_lo_ready = sem("lat_lo_ready")
        kv_hi_turned = sem("kv_hi_turned")
        kv_lo_turned = sem("kv_lo_turned")
        kv_hi_copied = sem("kv_hi_copied")
        kv_lo_copied = sem("kv_lo_copied")

        def lat(dst, m, c):
            cols = slice(c * CH, (c + 1) * CH)
            return qlatT[dst][:, m, cols] if m < KQ else kvT[dst][:, cols]

        def lat_scale(m):
            return SCALE if m < KQ else 1.0

        block = ctx.enter_context(nc.Block())

        @block.sync
        def _(sp):
            for c in range(NC):
                rows = slice(TC * c, TC * (c + 1))
                sp.dma_start(x[:, rows, :], hbm["x"].rearrange("(t p) d -> p t d", p=P)[:, rows, :]
                             ).then_inc(x_loaded[c], 16)
                if c == 0:
                    sp.dma_start(w_raw[:, :, 0:QR],
                                 hbm["Wq_down"].rearrange("(k p) n -> p k n", p=P)).then_inc(wlat_loaded, 16)
                    sp.dma_start(w_raw[:, :, QR:QR + KVR],
                                 hbm["Wkv_down"].rearrange("(k p) n -> p k n", p=P)).then_inc(wlat_loaded, 16)
                    sp.dma_start(ident[:], hbm["ident"]).then_inc(ident_loaded, 16)
            load_pair_weights(sp, hbm, pair_w, 0, pair_loaded)

        @block.vector
        def _(dve):
            def tile_stats(t):
                if t % TC == 0:
                    dve.wait_ge(x_loaded[t // TC], 16)
                nc.vector.bn_stats(bn[:, t % TC, :], x[:, t, :]).then_inc(stats_done, 1)

            def chunk_stats(c):
                for t in range(TC * c, TC * (c + 1)):
                    dve.wait_ge(stats_done, TC * 2 * c + t % TC + 1)
                    nc.vector.bn_aggr(mv[:, t, :], bn[:, t % TC, :]).then_inc(stats_done, 1)
                dve.wait_ge(stats_done, TC * 2 * (c + 1))
                rows = slice(TC * c, TC * (c + 1))
                nc.vector.tensor_scalar(std[:, rows], mv[:, rows, 1], LN_EPS, None, ALU.add).then_inc(var_ready, 1)
                dve.wait_ge(std_ready, c + 1)
                nc.vector.reciprocal(rstd[:, rows], std[:, rows]).then_inc(rstd_ready if c else rstd_done, 1)

            for c in range(AHEAD):
                for t in range(TC * c, TC * (c + 1)):
                    tile_stats(t)
                chunk_stats(c)
                if c == 0:
                    dve.wait_ge(rstd_done, 1)
                    for t in range(TC):
                        nc.vector.tensor_scalar(x[:, t, :], x[:, t, :], mv[:, t, 0:1], rstd[:, t:t + 1],
                                                ALU.subtract, ALU.mult).then_inc(xn_ready, 1)
            for c in range(NC + 2):
                for i in range(TC):
                    if c < NC:
                        t = TC * c + i
                        dve.wait_ge(xt_hi_ready, t + 1)
                        nc.vector.tensor_tensor(xT[1][:, :, t * P:(t + 1) * P],
                                                ps[:, t % 2, :].rearrange("p (k n) -> p k n", k=KD),
                                                xT[0][:, :, t * P:(t + 1) * P].bitcast(F32),
                                                ALU.subtract).then_inc(xt_lo_ready, 1)
                    if 1 <= c <= NC and i < NL:
                        dve.wait_ge(lat_hi_ready, NL * (c - 1) + i + 1)
                        nc.vector.scalar_tensor_tensor(lat(1, i, c - 1), ps[:, LAT0 + i, :], lat_scale(i),
                                                       lat(0, i, c - 1).bitcast(F32), ALU.mult,
                                                       ALU.subtract).then_inc(lat_lo_ready, 1)
                    if c + AHEAD < NC:
                        tile_stats(TC * (c + AHEAD) + i)
                if c >= 2:
                    dve.wait_ge(kv_lo_turned, c - 1)
                    nc.vector.tensor_copy(kv[1][:, TC * (c - 2):TC * (c - 1), :],
                                          ps[:, KV0 + 1, :].rearrange("p (t n) -> p t n", t=TC)
                                          ).then_inc(kv_lo_copied, 1)
                if c + AHEAD < NC:
                    chunk_stats(c + AHEAD)

        @block.gpsimd
        def _(pool):
            pool.wait_ge(wlat_hi_ready, 1)
            nc.gpsimd.tensor_tensor(w[1][:], w_raw[:], w[0][:].bitcast(F32), ALU.subtract).then_inc(wlat_lo_ready, 1)
            for c in range(1, NC):
                pool.wait_ge(rstd_ready, c)
                for t in range(TC * c, TC * (c + 1)):
                    nc.gpsimd.tensor_scalar(x[:, t, :], x[:, t, :], mv[:, t, 0:1], rstd[:, t:t + 1],
                                            ALU.subtract, ALU.mult).then_inc(xn_ready, 1)
            pool.wait_ge(pair_hi_ready, 1)
            for raw, hi, lo in pair_views(pair_w, 0):
                nc.gpsimd.tensor_tensor(lo, raw, hi.bitcast(F32), ALU.subtract)

        @block.scalar
        def _(act):
            def root(c):
                rows = slice(TC * c, TC * (c + 1))
                act.wait_ge(var_ready, c + 1)
                nc.scalar.activation(std[:, rows], std[:, rows], ACT.Sqrt).then_inc(std_ready, 1)

            for c in range(AHEAD):
                root(c)
                if c == 0:
                    act.wait_ge(wlat_loaded, 32)
                    nc.scalar.copy(w[0][:], w_raw[:]).then_inc(wlat_hi_ready, 1)
            for c in range(NC + 2):
                for i in range(TC):
                    if c < NC:
                        t = TC * c + i
                        act.wait_ge(xt_ready, t + 1)
                        nc.scalar.copy(xT[0][:, :, t * P:(t + 1) * P],
                                       ps[:, t % 2, :].rearrange("p (k n) -> p k n", k=KD)).then_inc(xt_hi_ready, 1)
                    if 1 <= c <= NC and i < NL:
                        act.wait_ge(lat_ready, NL * (c - 1) + i + 1)
                        nc.scalar.activation(lat(0, i, c - 1), ps[:, LAT0 + i, :], ACT.Copy,
                                             scale=lat_scale(i)).then_inc(lat_hi_ready, 1)
                if c >= 2:
                    act.wait_ge(kv_hi_turned, c - 1)
                    nc.scalar.copy(kv[0][:, TC * (c - 2):TC * (c - 1), :],
                                   ps[:, KV0, :].rearrange("p (t n) -> p t n", t=TC)).then_inc(kv_hi_copied, 1)
                if c + AHEAD < NC:
                    root(c + AHEAD)
                if c == SPLIT_AT:
                    act.wait_ge(pair_loaded, 16 * PAIR_LOADS)
                    for n, (raw, hi, _lo) in enumerate(pair_views(pair_w, 0)):
                        last = nc.scalar.copy(hi, raw)
                    last.then_inc(pair_hi_ready, 1)

        @block.tensor
        def _(pe):
            pe.wait_ge(ident_loaded, 16)
            for c in range(NC + 2):
                for i in range(TC):
                    if c < NC:
                        t = TC * c + i
                        pe.wait_ge(xn_ready, t + 1)
                        if t >= 2:
                            pe.wait_ge(xt_lo_ready, t - 1)
                        for k in range(KD):
                            last = nc.tensor.transpose(ps[:, t % 2, k * P:(k + 1) * P],
                                                       x[:, t, k * P:(k + 1) * P], ident[:, :])
                        last.then_inc(xt_ready, 1)
                    if 1 <= c <= NC and i < NL:
                        if i == 0:
                            pe.wait_ge(xt_lo_ready, TC * c)
                            if c == 1:
                                pe.wait_ge(wlat_lo_ready, 1)
                        if c > 1:
                            pe.wait_ge(lat_lo_ready, NL * (c - 2) + i + 1)
                        n = 0
                        for k in range(KD):
                            for a, b in parts(0, 1):
                                last = nc.tensor.matmul(ps[:, LAT0 + i, :], w[a][:, k, i * P:(i + 1) * P],
                                                        xT[b][:, k, (c - 1) * CH:c * CH],
                                                        start=(n == 0), stop=(n == 3 * KD - 1))
                                n += 1
                        last.then_inc(lat_ready, 1)
                if c >= 2:
                    pe.wait_ge(lat_lo_ready, NL * (c - 1))
                    for part, done, copied in ((0, kv_hi_turned, kv_hi_copied), (1, kv_lo_turned, kv_lo_copied)):
                        if c > 2:
                            pe.wait_ge(copied, c - 2)
                        for q in range(TC):
                            t = TC * (c - 2) + q
                            last = nc.tensor.transpose(ps[:, KV0 + part, q * P:(q + 1) * P],
                                                       kvT[part][:, t * P:(t + 1) * P].bitcast(F32), ident[:, :])
                        last.then_inc(done, 1)


def heads_inputs(nc, hbm, keep, pair_w, xT, qlatT, kvT):
    ident, abs_sums = keep["ident"], keep["abs_sums"]
    Q, K = 0, 1
    ROT = ((K, ROT_K, xT, KD), (Q, ROT_Q, qlatT, KQ))
    PLAIN = ((Q, PLAIN_Q, qlatT, KQ), (K, PLAIN_K, [z[:].rearrange("p (k n) -> p k n", k=1) for z in kvT], 1))
    PLAIN0, WV_BANK, WVO0 = 2, 4, 5
    with ExitStack() as ctx:
        def sb(name, shape, dt=F32):
            return ctx.enter_context(nc.sbuf_tensor(name, shape, dt))

        def sem(name):
            return ctx.enter_context(nc.semaphore(name))

        cos, sin = sb("cos", [P, T]), sb("sin", [P, T])
        w = pair_w["split"]
        wv_raw = sb("wv_raw", [P, 2, P])
        wvT = [sb(f"wvT_{n}", [P, 2, P], F32R) for n in ("hi", "lo")]
        wo_raw = sb("wo_raw", [P, 2, D])
        wo = [sb(f"wo_{n}", [P, 2, D], F32R) for n in ("hi", "lo")]
        wvo_out = sb("wvo_out", [P, 2, D])
        ternary_raw = sb("ternary_raw", [P, WCH])
        by_cos = sb("by_cos", [P, 2, CH])
        by_sin = sb("by_sin", [P, 2, CH])
        rot_out = sb("rot_out", [P, 2, CH])
        plain_out = sb("plain_out", [P, 2, CH])
        ps = ctx.enter_context(nc.psum_tensor("ps_proj", [P, 8, CH], F32))

        tables_loaded = [sem(f"tables_loaded{i}") for i in range(2)]
        w_loaded = sem("w_loaded")
        w_hi_ready = sem("w_hi_ready")
        w_lo_ready = sem("w_lo_ready")
        wo_hi_ready = sem("wo_hi_ready")
        wv_landed = sem("wv_landed")
        wv_turned = sem("wv_turned")
        wv_hi_ready = sem("wv_hi_ready")
        wv_lo_ready = sem("wv_lo_ready")
        wvo_ready = sem("wvo_ready")
        ternary_loaded = sem("ternary_loaded")
        abs_done = sem("abs_done")
        wvo_copied = sem("wvo_copied")
        rot_stored, plain_stored, wvo_stored = (keep[f"{n}_stored"] for n in ("rot", "plain", "wvo"))
        rot_ready = sem("rot_ready")
        rot_bank_free = sem("rot_bank_free")
        rot_taken = sem("rot_taken")
        multiplied = sem("multiplied")
        rot_summed = sem("rot_summed")
        products_free = sem("products_free")
        rot_done = sem("rot_done")
        plain_ready = sem("plain_ready")
        plain_bank_free = sem("plain_bank_free")
        plain_taken = sem("plain_taken")
        plain_done = sem("plain_done")

        NW = PAIR_LOADS + 2
        PER_PAIR = 2 * NC

        def load_weights(sp, pair):
            heads = bass.ds(pair * 2, 2)
            load_pair_weights(sp, hbm, pair_w, pair, w_loaded)
            sp.dma_start(wv_raw[:], hbm["Wv_up"].rearrange("p (h n) -> p h n", n=P)[:, heads, :]
                         ).then_inc(w_loaded, 16)
            sp.dma_start(wo_raw[:], hbm["Wo"].rearrange("(h p) n -> p h n", p=P)[:, heads, :]
                         ).then_inc(w_loaded, 16)

        def split_hi(j):
            for raw, hi, _lo in pair_views(pair_w, j):
                last = nc.scalar.copy(hi, raw)
            last.then_inc(w_hi_ready, 1)

        def split_lo(j):
            for raw, hi, lo in pair_views(pair_w, j):
                last = nc.gpsimd.tensor_tensor(lo, raw, hi.bitcast(F32), ALU.subtract)
            last.then_inc(w_lo_ready, 1)

        block = ctx.enter_context(nc.Block())

        @block.sync
        def _(sp):
            for n, toks in enumerate((slice(0, CH), slice(CH, T))):
                sp.dma_start(cos[:, toks], hbm["cos"][:, toks]).then_inc(tables_loaded[n], 16)
                sp.dma_start(sin[:, toks], hbm["sin"][:, toks]).then_inc(tables_loaded[n], 16)
            with sp.Fori(0, PAIRS // 2) as i:
                for j in range(2):
                    pair = 2 * i + j
                    following = sp.snap((pair + 1) % PAIRS)
                    load_weights(sp, following)
                    for c in range(NC):
                        toks = slice(c * CH, (c + 1) * CH)
                        for g in range(2):
                            sp.wait_ge(rot_done, PER_PAIR * j + 2 * c + g + 1)
                            sp.dma_start(hbm["rotT"][ROT[g][0], bass.ds(pair, 1), :, toks],
                                         rot_out[:, g, :]).then_inc(rot_stored[g], 16)
                        for g in range(2):
                            sp.wait_ge(plain_done, PER_PAIR * j + 2 * c + g + 1)
                            sp.dma_start(hbm["plainT"][PLAIN[g][0], bass.ds(pair, 1), :, toks],
                                         plain_out[:, g, :]).then_inc(plain_stored[g], 16)
                        if c < len(MATS):
                            sp.wait_ge(abs_done, len(MATS) * j + c + 1)
                            sp.dma_start(ternary_raw[:], weight_chunks(hbm[MATS[c]])[bass.ds(pair, 1), :, :]
                                         ).then_inc(ternary_loaded, 16)
                    sp.wait_ge(wvo_copied, j + 1)
                    sp.dma_start(hbm["wvo"].rearrange("(h p) n -> p h n", p=P)[:, bass.ds(2 * following, 2), :],
                                 wvo_out[:]).then_inc(wvo_stored, 16)
                sp.sem_inc(plain_done, -2 * PER_PAIR)
                sp.sem_inc(rot_done, -2 * PER_PAIR)
                sp.sem_inc(wvo_copied, -2)
                sp.sem_inc(abs_done, -2 * len(MATS))

        @block.scalar
        def _(act):
            for s in (*plain_stored, wvo_stored):
                act.sem_inc(s, 16)
            act.sem_inc(abs_done, 1)
            with act.Fori(0, PAIRS // 2) as i:
                for j in range(2):
                    for c in range(NC):
                        if c == NC - 1:
                            act.wait_ge(wv_turned, j + 1)
                            nc.scalar.copy(wvT[0][:], ps[:, WV_BANK, 0:2 * P].rearrange("p (h n) -> p h n", h=2)
                                           ).then_inc(wv_hi_ready, 1)
                        for g in range(2):
                            act.wait_ge(plain_ready, PER_PAIR * j + 2 * c + g + 1)
                            act.wait_ge(plain_stored[g], 16)
                            act.sem_inc(plain_stored[g], -16)
                            nc.scalar.copy(plain_out[:, g, :], ps[:, PLAIN0 + g, :]).then_inc(plain_taken, 1)
                            act.wait_ge(plain_taken, PER_PAIR * j + 2 * c + g + 1)
                            act.sem_inc(plain_bank_free, 1)
                            act.sem_inc(plain_done, 1)
                        if c > 0:
                            act.wait_ge(ternary_loaded, 16 * (len(MATS) * j + c))
                            nc.scalar.activation(ternary_raw[:], ternary_raw[:], ACT.Abs,
                                                 accum_out=abs_sums[:, c - 1, bass.ds(2 * i + j, 1)]
                                                 ).then_inc(abs_done, 1)
                        if c == 1:
                            act.wait_ge(w_loaded, 16 * NW * (j + 1))
                            act.sem_inc(wv_landed, 1)
                            split_hi(1 - j)
                            nc.scalar.copy(wo[0][:], wo_raw[:]).then_inc(wo_hi_ready, 1)
                    act.wait_ge(wvo_ready, j + 1)
                    act.wait_ge(wvo_stored, 16)
                    act.sem_inc(wvo_stored, -16)
                    nc.scalar.copy(wvo_out[:], ps[:, WVO0:WVO0 + 2, :]).then_inc(wvo_copied, 1)
                act.sem_inc(plain_ready, -2 * PER_PAIR)
                act.sem_inc(plain_taken, -2 * PER_PAIR)
                act.sem_inc(w_loaded, -2 * 16 * NW)
                act.sem_inc(wv_turned, -2)
                act.sem_inc(wvo_ready, -2)
                act.sem_inc(ternary_loaded, -2 * 16 * len(MATS))

        @block.gpsimd
        def _(pool):
            nc.gpsimd.memset(keep["ones"][:], 1.0)
            for s in rot_stored:
                pool.sem_inc(s, 16)
            with pool.Fori(0, PAIRS // 2) as i:
                for j in range(2):
                    for c in range(NC):
                        for g in range(2):
                            pool.wait_ge(multiplied, PER_PAIR * j + 2 * c + g + 1)
                            pool.wait_ge(rot_stored[g], 16)
                            pool.sem_inc(rot_stored[g], -16)
                            nc.gpsimd.tensor_tensor(rot_out[:, g, :], by_cos[:, g, :], by_sin[:, g, :],
                                                    ALU.add).then_inc(rot_summed, 1)
                            pool.wait_ge(rot_summed, PER_PAIR * j + 2 * c + g + 1)
                            pool.sem_inc(products_free, 1)
                            pool.sem_inc(rot_done, 1)
                        if c == 1:
                            pool.wait_ge(w_hi_ready, j + 1)
                            split_lo(1 - j)
                pool.sem_inc(multiplied, -2 * PER_PAIR)
                pool.sem_inc(rot_summed, -2 * PER_PAIR)
                pool.sem_inc(w_hi_ready, -2)

        @block.vector
        def _(dve):
            dve.wait_ge(tables_loaded[0], 32)
            dve.sem_inc(products_free, 2)
            half = P // 2
            with dve.Fori(0, PAIRS // 2) as i:
                for j in range(2):
                    for c in range(NC):
                        toks = slice(c * CH, (c + 1) * CH)
                        if c == 1:
                            dve.wait_ge(tables_loaded[1], 32)
                        if c == NC - 1:
                            dve.wait_ge(wv_hi_ready, j + 1)
                            nc.vector.tensor_tensor(wvT[1][:],
                                                    ps[:, WV_BANK, 0:2 * P].rearrange("p (h n) -> p h n", h=2),
                                                    wvT[0][:].bitcast(F32), ALU.subtract).then_inc(wv_lo_ready, 1)
                        for g in range(2):
                            dve.wait_ge(rot_ready, PER_PAIR * j + 2 * c + g + 1)
                            dve.wait_ge(products_free, PER_PAIR * j + 2 * c + g + 1)
                            nc.vector.tensor_tensor(by_cos[:, g, :], ps[:, g, :], cos[:, toks], ALU.mult)
                            nc.vector.tensor_tensor(by_sin[0:half, g, :], ps[half:P, g, :],
                                                    sin[half:P, toks], ALU.mult)
                            nc.vector.tensor_tensor(by_sin[half:P, g, :], ps[0:half, g, :],
                                                    sin[0:half, toks], ALU.mult).then_inc(rot_taken, 1)
                            dve.wait_ge(rot_taken, PER_PAIR * j + 2 * c + g + 1)
                            dve.sem_inc(rot_bank_free, 1)
                            dve.sem_inc(multiplied, 1)
                        if c == 2:
                            dve.wait_ge(wo_hi_ready, j + 1)
                            nc.vector.tensor_tensor(wo[1][:], wo_raw[:], wo[0][:].bitcast(F32), ALU.subtract)
                dve.sem_inc(rot_ready, -2 * PER_PAIR)
                dve.sem_inc(rot_taken, -2 * PER_PAIR)
                dve.sem_inc(products_free, -2 * PER_PAIR)
                dve.sem_inc(wv_hi_ready, -2)
                dve.sem_inc(wo_hi_ready, -2)

        @block.tensor
        def _(pe):
            pe.sem_inc(w_lo_ready, 1)
            pe.sem_inc(rot_bank_free, 2)
            pe.sem_inc(plain_bank_free, 2)
            with pe.Fori(0, PAIRS // 2) as i:
                for j in range(2):
                    pe.wait_ge(w_lo_ready, j + 1)

                    def product(bank, first, right, slices, toks):
                        n = 0
                        for k in range(slices):
                            for a, b in parts(0, 1):
                                mm = nc.tensor.matmul(ps[:, bank, :], w[j][a][:, first + k, :],
                                                      right[b][:, k, toks],
                                                      start=(n == 0), stop=(n == 3 * slices - 1))
                                n += 1
                        return mm

                    for c in range(NC):
                        toks = slice(c * CH, (c + 1) * CH)
                        if c == NC - 1:
                            pe.wait_ge(wv_landed, j + 1)
                            for h in range(2):
                                last = nc.tensor.transpose(ps[:, WV_BANK, h * P:(h + 1) * P],
                                                           wv_raw[:, h, :], ident[:, :])
                            last.then_inc(wv_turned, 1)
                        for g in range(2):
                            n = PER_PAIR * j + 2 * c + g + 1
                            pe.wait_ge(rot_bank_free, n)
                            product(g, *ROT[g][1:2], ROT[g][2], ROT[g][3], toks).then_inc(rot_ready, 1)
                        for g in range(2):
                            n = PER_PAIR * j + 2 * c + g + 1
                            pe.wait_ge(plain_bank_free, n)
                            product(PLAIN0 + g, *PLAIN[g][1:2], PLAIN[g][2], PLAIN[g][3],
                                    toks).then_inc(plain_ready, 1)
                    pe.wait_ge(wv_lo_ready, j + 1)
                    for h in range(2):
                        for n, (a, b) in enumerate(parts(0, 1)):
                            last = nc.tensor.matmul(ps[:, WVO0 + h, :], wvT[a][:, h, :], wo[b][:, h, :],
                                                    start=(n == 0), stop=(n == 2))
                    last.then_inc(wvo_ready, 1)
                pe.sem_inc(w_lo_ready, -2)
                pe.sem_inc(wv_landed, -2)
                pe.sem_inc(rot_bank_free, -2 * PER_PAIR)
                pe.sem_inc(plain_bank_free, -2 * PER_PAIR)
                pe.sem_inc(wv_lo_ready, -2)


QCH = 256
TPU = QCH // P
UPH = T // QCH
UNITS = 2 * UPH
PIECE = CH
RING = 4
SPLITS = 2 * NC + 1
FIRST = 3


def pieces(c, t):
    keys = c * QCH + (t + 1) * P
    return [(k, min(PIECE, keys - k)) for k in range(0, keys, PIECE)]


def npieces(c):
    return len(pieces(c, 0))


def attention_plan():
    steps = [(u, s) for u in range(UNITS) for s in range(u % UPH + 1)]
    first = [steps.index((u, 0)) for u in range(UNITS)]
    in_turn = {}
    for u in range(UNITS):
        n = u % UPH + 1
        for s in range(n):
            in_turn.setdefault(2 * u + 3 + (s >= (n + 2) // 2), []).append(first[u] + s)
    plan = []
    scored = softened = 0

    def soften(softmax, count):
        nonlocal softened
        for _ in range(min(count, len(softmax))):
            plan.append(softmax.pop(0))
            softened += 1

    for g in range(TPU * UNITS + 5):
        todo = in_turn.get(g, [])
        score, softmax, out = [], [], []
        if g < TPU * UNITS:
            u, t = divmod(g, TPU)
            score = [("scores", u, t, p) for p in range(npieces(u % UPH))]
        if 0 < g <= TPU * UNITS:
            u, t = divmod(g - 1, TPU)
            softmax = [("exp", u, t, p) for p in range(npieces(u % UPH))]
        if g >= 5:
            out = [("out", *divmod(g - 5, TPU))]
        at = []
        for p in range(len(score)):
            leaves = max(scored + p - RING + 1 - softened, 0)
            at.append(min(max(at[-1] + 1 if at else 0, leaves + 1 if leaves else 0), len(todo)))

        def score_next(k):
            nonlocal scored
            while score and at[0] <= k:
                soften(softmax, scored - RING + 1 - softened)
                plan.append(score.pop(0))
                at.pop(0)
                scored += 1

        if todo and todo[0] in first:
            if todo[0]:
                score_next(0)
                at = [max(x - 1, 0) for x in at]
            plan.append(("turn", todo[0], *steps[todo[0]]))
        for k, n in enumerate(todo + [None]):
            if n is not None and n + 1 < len(steps) and n + 1 not in first:
                plan.append(("turn", n + 1, *steps[n + 1]))
            soften(softmax, 2 if k == 0 else 1)
            score_next(k)
            if n in first and out:
                plan.append(out.pop(0))
            if n is not None:
                plan.append(("values", n, *steps[n]))
            if out:
                plan.append(out.pop(0))
            if n is not None and (n + 1 == len(steps) or n + 1 in first):
                plan.append(("sums", steps[n][0]))
        soften(softmax, len(softmax))
        j, c = divmod(g // TPU, UPH)
        k = TPU * (c - 3) + g % TPU
        if j < 2 and 0 <= k < SPLITS:
            plan.append(("split", j, k))
    return plan


def attention(nc, hbm, keep):
    y, kv, ident, scale, bound = (keep[n] for n in ("y", "kv", "ident", "scale", "bound"))
    abs_total = keep["abs_total"]
    plan = attention_plan()
    tile_pieces = [(u, t, p) for u in range(UNITS) for t in range(TPU) for p in range(npieces(u % UPH))]
    NPIECES = len(tile_pieces)
    NSTEPS = sum(e[0] == "values" for e in plan)
    piece_no = {x: n for n, x in enumerate(tile_pieces)}
    with ExitStack() as ctx:
        def sb(name, shape, dt=F32):
            return ctx.enter_context(nc.sbuf_tensor(name, shape, dt))

        def sem(name):
            return ctx.enter_context(nc.semaphore(name))

        k_raw, q_raw, w_raw = sb("k_raw", [P, T]), sb("q_raw", [P, T]), sb("wvo_raw", [P, D])
        k = [[sb(f"k_{n}{j}", [P, T], F32R) for n in ("hi", "lo")] for j in range(2)]
        q = [[sb(f"q_{n}{j}", [P, T], F32R) for n in ("hi", "lo")] for j in range(2)]
        w = [[sb(f"wvo_{n}{j}", [P, D], F32R) for n in ("hi", "lo")] for j in range(2)]
        probs = sb("probs", [P, 2, TPU, T])
        SLOTS = (2, 3)
        turned = [sb(f"turned_{n}", [P, 2 * SLOTS[part], 2 * QCH], F32R) for part, n in enumerate(("hi", "lo"))]
        o = [sb(f"o_{n}", [P, 2, QCH], F32R) for n in ("hi", "lo")]
        negmax = sb("negmax", [P, 2, RING])
        bias = sb("bias", [P, 2, TPU])
        sums = sb("sums", [P, 4, TPU, RING])
        total = sb("total", [P, 2, TPU])
        share = sb("share", [P, 2, TPU])
        sign_raw = sb("sign_raw", [P, WCH])
        below = sb("below", [P, WCH], BF16)
        signs = sb("signs", [P, WCH], BF16)
        mask_raw = sb("mask_raw", [P, P])
        mask = sb("mask", [P, P], BF16)
        identb = sb("identb", [P, P], BF16)

        ps_scores = ctx.enter_context(nc.psum_tensor("ps_scores", [P, RING, PIECE], F32))
        ps_turn = ctx.enter_context(nc.psum_tensor("ps_turn", [P, 2, 2 * QCH], F32))
        ps_o = ctx.enter_context(nc.psum_tensor("ps_o", [P, 2, D], F32))

        sign_loaded = sem("sign_loaded")
        compared = sem("compared")
        abs_summed, scale_done, bounds_ready = sem("abs_summed"), sem("scale_done"), sem("bounds_ready")
        signs_ready = sem("signs_ready")
        signs_stored = sem("signs_stored")
        y_loaded = [sem(f"y_loaded{m}") for m in range(NC)]
        mask_loaded = sem("mask_loaded")
        mask_ready = sem("mask_ready")
        stores_left = sem("stores_left")
        zeros_ready = sem("zeros_ready")
        k_loaded, q_loaded, w_loaded = sem("k_loaded"), sem("q_loaded"), sem("wvo_loaded")
        first_loaded = [sem(f"first_loaded{i}") for i in range(2)]
        first_hi_ready, first_lo_ready = sem("first_hi_ready"), sem("first_lo_ready")
        first_split = sem("first_split")
        raw_free = sem("raw_free")
        split_hi_ready = sem("split_hi_ready")
        split_ready = sem("split_ready")
        scores_ready = sem("scores_ready")
        max_done = sem("max_done")
        bias_ready = sem("bias_ready")
        exp_done = sem("exp_done")
        turn_ready = sem("turn_ready")
        turned_hi_ready = sem("turned_hi_ready")
        turned_hi_told = sem("turned_hi_told")
        turned_lo_ready = sem("turned_lo_ready")
        o_ready = sem("o_ready")
        o_hi_ready = sem("o_hi_ready")
        o_lo_ready = sem("o_lo_ready")
        out_ready = sem("out_ready")
        share_done = sem("share_done")
        out_added = sem("out_added")

        def out_bank(u, t):
            return t if u == UNITS - 1 else u % 2

        def last_step(u, s):
            return s == u % UPH

        def slot(part, n, u, s):
            return n % SLOTS[part] + SLOTS[part] * last_step(u, s)

        def turned_part(part, n, u, s):
            return turned[part][:, slot(part, n, u, s), P * last_step(u, s):]

        def turned_psum(n, u, s):
            return ps_turn[:, n % 2, P * last_step(u, s):]

        def bias_of(u, t):
            return bias[:, u % 2, t:t + 1]

        def load_qk(sp, pair, head, n, toks, done):
            pr, raw = bass.ds(pair, 1), (q_raw, k_raw)[n]
            sp.dma_start(raw[0:ND, toks], hbm["plainT"][n, pr, ND * head:ND * (head + 1), toks]).then_inc(done, 16)
            for f in range(2):
                r = P // 2 * f + HALF * head
                sp.dma_start(raw[ND + HALF * f:ND + HALF * (f + 1), toks],
                             hbm["rotT"][n, pr, r:r + HALF, toks]).then_inc(done, 16)

        def load_wvo(sp, pair, head, done):
            sp.dma_start(w_raw[:], hbm["wvo"].rearrange("(q h p) n -> q h p n", h=2, p=P)[bass.ds(pair, 1), head, :, :]
                         ).then_inc(done, 16)

        def load_head(sp, pair, head):
            load_wvo(sp, pair, head, w_loaded)
            load_qk(sp, pair, head, 1, slice(0, T), k_loaded)
            load_qk(sp, pair, head, 0, slice(0, T), q_loaded)

        def split_views(j, n):
            if n == 0:
                return w_raw[:], w[j][0][:], w[j][1][:]
            raw, (hi, lo) = (k_raw, k[j]) if n % 2 else (q_raw, q[j])
            cols = slice((n - 1) // 2 * CH, ((n - 1) // 2 + 1) * CH)
            return raw[:, cols], hi[:, cols], lo[:, cols]

        def split_hi(act, j, n, heads_before):
            if n < 3:
                loaded, loads = ((w_loaded, 1), (k_loaded, 3), (q_loaded, 3))[n]
                act.wait_ge(loaded, 16 * loads * (heads_before + 1))
            raw, hi, _ = split_views(j, n)
            nc.scalar.copy(hi, raw).then_inc(split_hi_ready, 1)

        def split_lo(pool, j, n, before):
            pool.wait_ge(split_hi_ready, before + n + 1)
            raw, hi, lo = split_views(j, n)
            nc.gpsimd.tensor_tensor(lo, raw, hi.bitcast(F32), ALU.subtract).then_inc(split_ready, 1)

        AHEAD = ((0, 0, 0), (0, 1, 0))
        SIGNS = ((0, 1), (2,))

        def make_signs(pool, m):
            pool.wait_ge(sign_loaded, 16 * (m + 1))
            nc.gpsimd.tensor_scalar(below[:], sign_raw[:], bound[:, 1, m:m + 1], None, ALU.is_lt)
            pool.wait_ge(signs_stored, 16 * (m + 1))
            nc.gpsimd.tensor_scalar(signs[:], sign_raw[:], bound[:, 0, m:m + 1], None, ALU.is_gt
                                    ).then_inc(compared, 1)
            pool.wait_ge(compared, m + 1)
            nc.gpsimd.tensor_tensor(signs[:], signs[:], below[:], ALU.subtract).then_inc(signs_ready, 1)

        def load_chunk(sp, m, pair):
            sp.dma_start(sign_raw[:], weight_chunks(hbm[MATS[m]])[bass.ds(pair, 1), :, :]).then_inc(sign_loaded, 16)

        block = ctx.enter_context(nc.Block())

        @block.sync
        def _(sp):
            for n in (1, 0):
                load_qk(sp, 0, 0, n, slice(0, CH), first_loaded[0])
            for s in (*keep["rot_stored"], *keep["plain_stored"], keep["wvo_stored"]):
                sp.wait_ge(s, 16)
            sp.sem_inc(stores_left, 1)
            load_wvo(sp, 0, 0, first_loaded[0])
            sp.dma_start(mask_raw[:], hbm["mask"]).then_inc(mask_loaded, 16)
            for n in (1, 0):
                load_qk(sp, 0, 0, n, slice(CH, T), first_loaded[1])
            load_chunk(sp, 0, 0)
            for m in range(NC):
                rows = slice(TC * m, TC * (m + 1))
                sp.dma_start(y[:, rows, :], hbm["x"].rearrange("(t p) d -> p t d", p=P)[:, rows, :]
                             ).then_inc(y_loaded[m], 16)
            sp.wait_ge(first_split, 1)
            with sp.Fori(0, PAIRS) as i:
                for j in range(2):
                    sp.wait_ge(raw_free, j + 1)
                    following = sp.snap((i + 1) % PAIRS)
                    load_head(sp, i if j == 0 else following, 1 - j)
                    for m in SIGNS[j]:
                        sp.wait_ge(signs_ready, m + 1)
                        sp.dma_start(weight_chunks(hbm["signs"][m])[bass.ds(i, 1), :, :], signs[:]
                                     ).then_inc(signs_stored, 16)
                        load_chunk(sp, (m + 1) % len(MATS), i if m + 1 < len(MATS) else following)
                sp.sem_inc(raw_free, -2)
                sp.sem_inc(signs_ready, -len(MATS))

        @block.gpsimd
        def _(pool):
            pool.wait_ge(bounds_ready, 2)
            pool.wait_ge(stores_left, 1)
            for part in range(2):
                nc.gpsimd.memset(turned[part][:, SLOTS[part]:, 0:P].bitcast(F32), 0.0).then_inc(zeros_ready, 1)
            for n in range(FIRST, SPLITS):
                split_lo(pool, 0, n, -FIRST)
            pool.sem_inc(split_hi_ready, FIRST - SPLITS)
            pool.drain().then_inc(raw_free, 1)
            pool.sem_inc(signs_stored, 16)
            with pool.Fori(0, PAIRS) as i:
                for j in range(2):
                    for m in SIGNS[j]:
                        make_signs(pool, m)
                    for n in range(SPLITS):
                        split_lo(pool, 1 - j, n, SPLITS * j)
                    pool.drain().then_inc(raw_free, 1)
                pool.sem_inc(split_hi_ready, -2 * SPLITS)
                pool.sem_inc(sign_loaded, -16 * len(MATS))
                pool.sem_inc(compared, -len(MATS))
                pool.sem_inc(signs_stored, -16 * len(MATS))
            pool.wait_ge(signs_stored, 16)
            pool.wait_ge(sign_loaded, 16)

        @block.scalar
        def _(act):
            def exponential(u, t, p, following=0):
                n = piece_no[u, t, p]
                first_key, keys = pieces(u % UPH, t)[p]
                act.wait_ge(bias_ready, TPU * (UNITS * following + u) + t + 1)
                nc.scalar.activation(probs[:, u % 2, t, first_key:first_key + keys],
                                     ps_scores[:, n % RING, 0:keys], ACT.Exp,
                                     bias=bias_of(u, t),
                                     accum_out=sums[:, u % 4, t, p:p + 1]).then_inc(exp_done, 1)

            act.wait_ge(first_loaded[0], 16 * 7)
            for n in range(FIRST):
                raw, hi, _ = split_views(0, n)
                nc.scalar.copy(hi, raw).then_inc(first_hi_ready, 1)
            act.wait_ge(mask_loaded, 16)
            nc.scalar.copy(mask[:], mask_raw[:])
            nc.scalar.copy(identb[:], ident[:]).then_inc(mask_ready, 1)
            for args in AHEAD:
                exponential(*args)
            act.wait_ge(first_loaded[1], 16 * 6)
            for n in range(FIRST, SPLITS):
                raw, hi, _ = split_views(0, n)
                nc.scalar.copy(hi, raw).then_inc(split_hi_ready, 1)
            with act.Fori(0, PAIRS) as i:
                for kind, *args in plan:
                    if kind == "split":
                        j, n = args
                        split_hi(act, 1 - j, n, j)
                    if kind == "exp" and tuple(args) not in AHEAD:
                        exponential(*args)
                    if kind == "turn":
                        n, u, s = args
                        act.wait_ge(turn_ready, n + 1)
                        nc.scalar.copy(turned_part(0, n, u, s), turned_psum(n, u, s)).then_inc(turned_hi_ready, 1)
                    if kind == "sums":
                        u, = args
                        act.wait_ge(o_ready, u + 1)
                        nc.scalar.copy(o[0][:, u % 2, :], ps_o[:, u % 2, 0:QCH]).then_inc(o_hi_ready, 1)
                        if u == UNITS - 1:
                            for first_args in AHEAD:
                                exponential(*first_args, following=1)
                act.sem_inc(k_loaded, -96)
                act.sem_inc(q_loaded, -96)
                act.sem_inc(w_loaded, -32)
                act.sem_inc(bias_ready, -TPU * UNITS)
                act.sem_inc(turn_ready, -NSTEPS)
                act.sem_inc(o_ready, -UNITS)

        @block.vector
        def _(dve):
            dve.wait_ge(abs_summed, 1)
            summed = ps_turn[:, 0, 0:len(MATS) * PAIRS].rearrange("p (m c) -> p m c", c=PAIRS)
            nc.vector.tensor_reduce(abs_total[:], summed, AX_X, ALU.add).then_inc(scale_done, 1)
            dve.wait_ge(scale_done, 1)
            nc.vector.tensor_scalar(scale[:], abs_total[:], 1.0 / (D * E), QUANT_EPS,
                                    ALU.mult, ALU.add).then_inc(scale_done, 1)
            dve.wait_ge(scale_done, 2)
            for n, half in enumerate((0.5, -0.5)):
                nc.vector.tensor_scalar(bound[:, n, :], scale[:], half, None, ALU.mult).then_inc(bounds_ready, 1)
            for n in range(FIRST):
                dve.wait_ge(first_hi_ready, n + 1)
                raw, hi, lo = split_views(0, n)
                nc.vector.tensor_tensor(lo, raw, hi.bitcast(F32), ALU.subtract).then_inc(first_lo_ready, 1)

            def only_maximum(u, t, p, following=0):
                n = piece_no[u, t, p]
                dve.wait_ge(scores_ready, NPIECES * following + n + 1)
                nc.vector.tensor_reduce(bias_of(u, t), ps_scores[:, n % RING, 0:pieces(u % UPH, t)[p][1]], AX_X,
                                        ALU.max, negate=True).then_inc(bias_ready, 1)

            for args in AHEAD:
                only_maximum(*args)
            with dve.Fori(0, PAIRS) as i:
                maxima = 0
                for kind, *args in plan:
                    if kind == "scores" and tuple(args) not in AHEAD:
                        u, t, p = args
                        tile = pieces(u % UPH, t)
                        n = piece_no[u, t, p]
                        dve.wait_ge(scores_ready, n + 1)
                        whole = len(tile) == 1
                        put = bias_of(u, t) if whole else negmax[:, t, p:p + 1]
                        nc.vector.tensor_reduce(put, ps_scores[:, n % RING, 0:tile[p][1]], AX_X, ALU.max,
                                                negate=True).then_inc(bias_ready if whole else max_done, 1)
                        if p + 1 == len(tile) and not whole:
                            maxima += len(tile)
                            dve.wait_ge(max_done, maxima)
                            nc.vector.tensor_reduce(bias_of(u, t), negmax[:, t, 0:len(tile)], AX_X, ALU.min
                                                    ).then_inc(bias_ready, 1)
                    if kind == "turn":
                        n, u, s = args
                        dve.wait_ge(turned_hi_ready, n + 1)
                        dve.sem_inc(turned_hi_told, 1)
                        nc.vector.tensor_tensor(turned_part(1, n, u, s), turned_psum(n, u, s),
                                                turned_part(0, n, u, s).bitcast(F32),
                                                ALU.subtract).then_inc(turned_lo_ready, 1)
                    if kind == "sums":
                        u, = args
                        dve.wait_ge(o_hi_ready, u + 1)
                        nc.vector.tensor_tensor(o[1][:, u % 2, :], ps_o[:, u % 2, 0:QCH],
                                                o[0][:, u % 2, :].bitcast(F32), ALU.subtract).then_inc(o_lo_ready, 1)
                        if u == UNITS - 1:
                            for first_args in AHEAD:
                                only_maximum(*first_args, following=1)
                    if kind == "out":
                        u, t = args
                        dve.wait_ge(out_ready, TPU * u + t + 1)
                        if t == 0:
                            nc.vector.tensor_reduce(total[:, u % 2, :], sums[:, u % 4, :, 0:npieces(u % UPH)],
                                                    AX_X, ALU.add).then_inc(share_done, 1)
                            dve.wait_ge(share_done, 2 * u + 1)
                            nc.vector.reciprocal(share[:, u % 2, :], total[:, u % 2, :]).then_inc(share_done, 1)
                            dve.wait_ge(share_done, 2 * u + 2)
                        row = TPU * (u % UPH) + t
                        if u < UPH and row % TC == 0:
                            dve.wait_ge(y_loaded[row // TC], 16)
                        nc.vector.scalar_tensor_tensor(y[:, row, :], ps_o[:, out_bank(u, t), :],
                                                       share[:, u % 2, t:t + 1], y[:, row, :],
                                                       ALU.mult, ALU.add).then_inc(out_added, 1)
                dve.sem_inc(scores_ready, -NPIECES)
                dve.sem_inc(max_done, -maxima)
                dve.sem_inc(turned_hi_ready, -NSTEPS)
                dve.sem_inc(o_hi_ready, -UNITS)
                dve.sem_inc(out_ready, -TPU * UNITS)
                dve.sem_inc(share_done, -2 * UNITS)

        @block.tensor
        def _(pe):
            nc.tensor.matmul(ps_turn[:, 0, 0:len(MATS) * PAIRS], keep["ones"][:],
                             keep["abs_sums"][:].rearrange("p m c -> p (m c)"),
                             start=True, stop=True).then_inc(abs_summed, 1)
            pe.wait_ge(mask_ready, 1)
            pe.wait_ge(zeros_ready, 2)
            pe.sem_inc(exp_done, RING)
            pe.wait_ge(first_lo_ready, FIRST)
            pe.sem_inc(split_ready, FIRST)
            pe.sem_inc(first_split, 1)
            pe.sem_inc(turned_lo_ready, 2)
            pe.sem_inc(out_added, 2)

            def score(u, t, p, following=0):
                j, c = divmod(u, UPH)
                n = piece_no[u, t, p]
                first_key, keys = pieces(c, t)[p]
                row = TPU * c + t
                if c % 2 == 0 and (t, p) == (0, 0):
                    pe.wait_ge(split_ready, SPLITS * (j + 2 * following) + FIRST + c)
                pe.wait_ge(exp_done, NPIECES * following + n + 1)
                diagonal = first_key + keys == (row + 1) * P
                cols = max(keys, QCH)
                for m, (x, z) in enumerate(parts(0, 1)):
                    last = nc.tensor.matmul(ps_scores[:, n % RING, 0:cols], q[j][x][:, row * P:(row + 1) * P],
                                            k[j][z][:, first_key:first_key + cols],
                                            start=(m == 0), stop=(m == 2 and not diagonal))
                if diagonal:
                    last = nc.tensor.matmul(ps_scores[:, n % RING, keys - P:keys], identb[:], mask[:],
                                            start=False, stop=True)
                last.then_inc(scores_ready, 1)

            def value(n, u, s, x, z, kb, start, stop):
                return nc.tensor.matmul(ps_o[:, u % 2, 0:QCH], kv[x][:, 2 * s + kb, :],
                                        turned[z][:, slot(z, n, u, s), (1 - kb) * QCH:(2 - kb) * QCH],
                                        start=start, stop=stop)

            for args in AHEAD:
                score(*args)
            with pe.Fori(0, PAIRS) as i:
                for kind, *args in plan:
                    if kind == "scores":
                        if tuple(args) not in AHEAD:
                            score(*args)
                    if kind == "turn":
                        n, u, s = args
                        if s == 0:
                            pe.wait_ge(exp_done, RING + piece_no[u, TPU - 1, npieces(u % UPH) - 1] + 1)
                        pe.wait_ge(turned_lo_ready, n + 1)
                        for at, (kb, t) in enumerate(((1, 0), (1, 1), (0, 0), (0, 1))):
                            if last_step(u, s) and at == 0:
                                continue
                            key = (2 * s + kb) * P
                            last = nc.tensor.transpose(ps_turn[:, n % 2, at * P:(at + 1) * P],
                                                       probs[:, u % 2, t, key:key + P], ident[:])
                        last.then_inc(turn_ready, 1)
                    if kind == "values":
                        n, u, s = args
                        if s == 0:
                            pe.wait_ge(out_added, 2 + TPU * (u - 1) if u > 1 else u + 1)
                        pe.wait_ge(turned_hi_told, n + 1)
                        for x in range(2):
                            for kb in range(2):
                                value(n, u, s, x, 0, kb, start=(s == 0 and (x, kb) == (0, 0)), stop=False)
                        for before in ([1] if s else []) + ([0] if last_step(u, s) else []):
                            pe.wait_ge(turned_lo_ready, 2 + n - before + 1)
                            for kb in range(2):
                                last = value(n - before, u, s - before, 0, 1, kb, start=False,
                                             stop=(before == 0 and kb == 1))
                        if last_step(u, s):
                            last.then_inc(o_ready, 1)
                    if kind == "out":
                        u, t = args
                        if (u, t) == (UNITS - 1, 0):
                            for first_args in AHEAD:
                                score(*first_args, following=1)
                        if t == 0 and u % UPH == 0:
                            pe.wait_ge(split_ready, SPLITS * (u // UPH) + 1)
                        if t == 0:
                            pe.wait_ge(o_lo_ready, u + 1)
                        if (t == 0) == (u == UNITS - 1):
                            pe.wait_ge(out_added, 2 + TPU * u + t)
                        for m, (x, z) in enumerate(parts(0, 1)):
                            last = nc.tensor.matmul(ps_o[:, out_bank(u, t), :],
                                                    o[x][:, u % 2, t * P:(t + 1) * P], w[u // UPH][z][:],
                                                    start=(m == 0), stop=(m == 2))
                        last.then_inc(out_ready, 1)
                pe.sem_inc(split_ready, -2 * SPLITS)
                pe.sem_inc(exp_done, -NPIECES)
                pe.sem_inc(turned_hi_told, -NSTEPS)
                pe.sem_inc(turned_lo_ready, -NSTEPS)
                pe.sem_inc(o_lo_ready, -UNITS)
                pe.sem_inc(out_added, -TPU * UNITS)



def turn_signs(nc, hbm, keep, ffn):
    y, ident = keep["y"], keep["ident"]
    wT, mv, rstd = ffn["wT"], ffn["mv"], ffn["rstd"]
    LOADS = 4
    GROUPS = 4
    BANKS = 8
    quarters = [(m, g) for m in range(len(MATS)) for g in range(LOADS)]
    with ExitStack() as ctx:
        def sb(name, shape, dt=F32):
            return ctx.enter_context(nc.sbuf_tensor(name, shape, dt))

        def sem(name):
            return ctx.enter_context(nc.semaphore(name))

        signs = sb("signs_in", [P, len(quarters), D * E // P // LOADS], BF16)
        identb = sb("identb3", [P, P], BF16)
        bn = sb("bn3", [P, 2, 6])
        std = sb("std3", [P, NT])
        ps_turn = ctx.enter_context(nc.psum_tensor("ps_signs", [P, BANKS, 2 * CH], BF16))

        loaded = [sem(f"signs_loaded{q}") for q in range(len(quarters))]
        identb_ready = sem("identb_ready")
        stats_done = sem("stats3_done")
        var_ready = sem("var3_ready")
        std_ready = sem("std3_ready")
        turned = [sem(f"signs_turned_{e}") for e in ("act", "dve")]
        copied = [sem(f"signs_copied_{e}") for e in ("act", "dve")]

        def owner(n):
            return int(n >= 18 and n % 2)

        owners = [owner(n) for n in range(GROUPS * len(quarters))]

        def place(n):
            (m, q), b = quarters[n // GROUPS], n % GROUPS
            turned = ps_turn[:, n % BANKS, 0:CH]
            if m < 2:
                return wT[m][:, b, q * CH:(q + 1) * CH], turned
            return wT[m][:, GROUPS * b:GROUPS * (b + 1), q * P:(q + 1) * P], turned.rearrange("p (e n) -> p e n", e=4)

        block = ctx.enter_context(nc.Block())

        @block.sync
        def _(sp):
            for at, (m, q) in enumerate(quarters):
                rows, width = (E, D) if m < 2 else (D, E)
                n = rows // P // LOADS
                source = hbm["signs"][m].rearrange("a b -> (a b)").rearrange("(r p n) -> p r n", p=P, n=width)
                sp.dma_start(signs[:, at, :].rearrange("p (r n) -> p r n", r=n),
                             source[:, n * q:n * (q + 1), :]).then_inc(loaded[at], 16)

        @block.scalar
        def _(act):
            nc.scalar.copy(identb[:], ident[:]).then_inc(identb_ready, 1)
            done = 0
            for n, who in enumerate(owners):
                if who == 0:
                    done += 1
                    act.wait_ge(turned[0], done)
                    put, psum = place(n)
                    nc.scalar.copy(put, psum).then_inc(copied[0], 1)
            act.wait_ge(var_ready, 1)
            nc.scalar.activation(std[:], std[:], ACT.Sqrt).then_inc(std_ready, 1)

        @block.vector
        def _(dve):
            for t in range(NT):
                nc.vector.bn_stats(bn[:, t % 2, :], y[:, t, :]).then_inc(stats_done, 1)
                dve.wait_ge(stats_done, 2 * t + 1)
                nc.vector.bn_aggr(mv[:, t, :], bn[:, t % 2, :]).then_inc(stats_done, 1)
            dve.wait_ge(stats_done, 2 * NT)
            nc.vector.tensor_scalar(std[:], mv[:, :, 1], LN_EPS, None, ALU.add).then_inc(var_ready, 1)
            done = 0
            for n, who in enumerate(owners):
                if who == 1:
                    done += 1
                    dve.wait_ge(turned[1], done)
                    put, psum = place(n)
                    nc.vector.tensor_copy(put, psum).then_inc(copied[1], 1)
            dve.wait_ge(std_ready, 1)
            nc.vector.reciprocal(rstd[:], std[:])

        @block.tensor
        def _(pe):
            pe.wait_ge(identb_ready, 1)
            for n, who in enumerate(owners):
                (m, q), b = quarters[n // GROUPS], n % GROUPS
                if b == 0:
                    pe.wait_ge(loaded[n // GROUPS], 16)
                if n >= BANKS:
                    before = owners[n - BANKS]
                    pe.wait_ge(copied[before], owners[:n - BANKS + 1].count(before))
                for r in range(4):
                    at = (r * D + b * P) if m < 2 else (4 * b + r) * P
                    last = nc.tensor.transpose(ps_turn[:, n % BANKS, r * P:(r + 1) * P],
                                               signs[:, n // GROUPS, at:at + P], identb[:])
                last.then_inc(turned[who], 1)


def feed_forward(nc, hbm, keep, ffn, out):
    y, ident = keep["y"], keep["ident"]
    wT, scale, mv, rstd = ffn["wT"], keep["scale"], ffn["mv"], ffn["rstd"]
    UP, GATE, DOWN = range(3)
    NORM_AT = {2 + 3 * t: t for t in range(TC)}
    with ExitStack() as ctx:
        def sb(name, shape, dt=F32):
            return ctx.enter_context(nc.sbuf_tensor(name, shape, dt))

        def sem(name):
            return ctx.enter_context(nc.semaphore(name))

        xn = sb("xn3", [P, 2, D])
        hT = [sb(f"hT_{n}", [P, 2, KD, CH], F32R) for n in ("hi", "lo")]
        gated = sb("gated", [P, CH])
        hidden = sb("hidden", [P, CH])
        hid = [sb(f"hidden_{n}", [P, 2, CH], F32R) for n in ("hi", "lo")]
        result = sb("result", [P, TC, D])
        ps_acc = ctx.enter_context(nc.psum_tensor("ps_acc", [P, TC, D], F32))
        ps_up = ctx.enter_context(nc.psum_tensor("ps_up", [P, 2, CH], F32))
        ps_gate = ctx.enter_context(nc.psum_tensor("ps_gate", [P, CH], F32))
        ps_turn = ctx.enter_context(nc.psum_tensor("ps_turn3", [P, D], F32))

        xn_ready = sem("xn3_ready")
        turn_ready = sem("turn3_ready")
        h_hi_ready = sem("h_hi_ready")
        h_lo_ready = sem("h_lo_ready")
        up_ready = sem("up_ready")
        silu_ready = sem("silu_ready")
        gate_ready = sem("gate_ready")
        hidden_ready = sem("hidden_ready")
        hid_hi_ready = sem("hid_hi_ready")
        hid_lo_ready = sem("hid_lo_ready")
        acc_ready = sem("acc_ready")
        result_ready = sem("result_ready")
        acc_free = sem("acc_free")
        stored = [sem(f"stored{t}") for t in range(TC)]

        block = ctx.enter_context(nc.Block())

        def h_tile(part, slot, t):
            return hT[part][:, bass.ds(slot, 1), :, t * P:(t + 1) * P]

        def slices(psum):
            return psum.rearrange("p (k n) -> p k n", k=KD)

        @block.vector
        def _(dve):
            def normalise(chunk, t, put):
                row = bass.ds(chunk * TC + t, 1)
                nc.vector.tensor_scalar(put, y[:, row, :], mv[:, row, 0], rstd[:, row],
                                        ALU.subtract, ALU.mult).then_inc(xn_ready, 1)

            def h_low(slot, t, psum):
                dve.wait_ge(h_hi_ready, t + 1)
                nc.vector.tensor_tensor(h_tile(1, slot, t), slices(psum), h_tile(0, slot, t).bitcast(F32),
                                        ALU.subtract).then_inc(h_lo_ready, 1)

            for t in range(TC):
                normalise(0, t, result[:, t, :])
            for t in range(TC):
                h_low(0, t, ps_acc[:, t, :])
            dve.sem_inc(h_hi_ready, -TC)
            for s in stored:
                dve.sem_inc(s, 16)
            with dve.Fori(0, NC) as i:
                following, slot = dve.snap((i + 1) % NC), dve.snap((i + 1) % 2)
                for e in range(ET):
                    if e in NORM_AT:
                        normalise(following, NORM_AT[e], xn[:, NORM_AT[e] % 2, :])
                    dve.wait_ge(silu_ready, e + 1)
                    dve.wait_ge(gate_ready, e + 1)
                    nc.vector.scalar_tensor_tensor(hidden[:], ps_gate[:], scale[:, GATE:GATE + 1], gated[:],
                                                   ALU.mult, ALU.mult).then_inc(hidden_ready, 1)
                    dve.wait_ge(hid_hi_ready, e + 1)
                    nc.vector.tensor_tensor(hid[1][:, e % 2, :], hidden[:], hid[0][:, e % 2, :].bitcast(F32),
                                            ALU.subtract).then_inc(hid_lo_ready, 1)
                    if e in NORM_AT:
                        h_low(slot, NORM_AT[e], ps_turn[:])
                for t in range(TC):
                    dve.wait_ge(acc_ready, t + 1)
                    dve.wait_ge(stored[t], 16)
                    dve.sem_inc(stored[t], -16)
                    nc.vector.scalar_tensor_tensor(result[:, t, :], ps_acc[:, t, :], scale[:, DOWN:DOWN + 1],
                                                   y[:, bass.ds(i * TC + t, 1), :].rearrange("p a n -> p (a n)"),
                                                   ALU.mult, ALU.add).then_inc(result_ready, 1)
                dve.sem_inc(silu_ready, -ET)
                dve.sem_inc(gate_ready, -ET)
                dve.sem_inc(hid_hi_ready, -ET)
                dve.sem_inc(h_hi_ready, -TC)
                dve.sem_inc(acc_ready, -TC)
            for s in stored:
                dve.wait_ge(s, 16)

        @block.sync
        def _(sp):
            with sp.Fori(0, NC) as i:
                for t in range(TC):
                    sp.wait_ge(result_ready, t + 1)
                    sp.sem_inc(acc_free, 1)
                    sp.dma_start(out.rearrange("(t p) d -> t p d", p=P)[bass.ds(i * TC + t, 1), :, :],
                                 result[:, t, :]).then_inc(stored[t], 16)
                sp.sem_inc(result_ready, -TC)

        @block.scalar
        def _(act):
            def h_high(slot, t, psum):
                act.wait_ge(turn_ready, t + 1)
                nc.scalar.copy(h_tile(0, slot, t), slices(psum)).then_inc(h_hi_ready, 1)

            for t in range(TC):
                h_high(0, t, ps_acc[:, t, :])
            act.sem_inc(turn_ready, -TC)
            with act.Fori(0, NC) as i:
                slot = act.snap((i + 1) % 2)
                for e in range(ET):
                    act.wait_ge(up_ready, e + 1)
                    nc.scalar.activation(gated[:], ps_up[:, e % 2, :], ACT.Silu, scale=scale[:, UP:UP + 1]
                                         ).then_inc(silu_ready, 1)
                    act.wait_ge(hidden_ready, e + 1)
                    nc.scalar.copy(hid[0][:, e % 2, :], hidden[:]).then_inc(hid_hi_ready, 1)
                    if e in NORM_AT:
                        h_high(slot, NORM_AT[e], ps_turn[:])
                act.sem_inc(up_ready, -ET)
                act.sem_inc(hidden_ready, -ET)
                act.sem_inc(turn_ready, -TC)

        @block.tensor
        def _(pe):
            def turn(t, source, psum):
                pe.wait_ge(xn_ready, t + 1)
                for k in range(KD):
                    last = nc.tensor.transpose(psum[:, k * P:(k + 1) * P], source[:, k * P:(k + 1) * P], ident[:])
                last.then_inc(turn_ready, 1)

            def down(e):
                pe.wait_ge(hid_lo_ready, e + 1)
                for t in range(TC):
                    if e == 0:
                        pe.wait_ge(acc_free, t + 1)
                    for part in range(2):
                        last = nc.tensor.matmul(ps_acc[:, t, :], hid[part][:, e % 2, t * P:(t + 1) * P],
                                                wT[DOWN][:, e, :], start=(e == 0 and part == 0),
                                                stop=(e == ET - 1 and part == 1))
                    if e == ET - 1:
                        last.then_inc(acc_ready, 1)

            for t in range(TC):
                turn(t, result[:, t, :], ps_acc[:, t, :])
            pe.sem_inc(xn_ready, -TC)
            pe.sem_inc(acc_free, TC)
            with pe.Fori(0, NC) as i:
                slot = pe.snap(i % 2)
                pe.wait_ge(h_lo_ready, TC)
                for e in range(ET):
                    for m, bank, ready in ((UP, ps_up[:, e % 2, :], up_ready), (GATE, ps_gate[:], gate_ready)):
                        before = e - 1 if m == UP else e
                        if before > 0:
                            pe.wait_ge(hid_lo_ready, before)
                        for kk in range(KD):
                            for part in range(2):
                                last = nc.tensor.matmul(bank, wT[m][:, kk, e * P:(e + 1) * P],
                                                        hT[part][:, bass.ds(slot, 1), kk, :],
                                                        start=(kk == 0 and part == 0),
                                                        stop=(kk == KD - 1 and part == 1))
                        last.then_inc(ready, 1)
                    if e:
                        down(e - 1)
                    if e in NORM_AT:
                        turn(NORM_AT[e], xn[:, NORM_AT[e] % 2, :], ps_turn[:])
                down(ET - 1)
                pe.sem_inc(h_lo_ready, -TC)
                pe.sem_inc(hid_lo_ready, -ET)
                pe.sem_inc(acc_free, -TC)
                pe.sem_inc(xn_ready, -TC)


def program(nc, hbm, out):
    hbm["plainT"] = nc.dram_tensor("plainT", [2, PAIRS, P, T], F32, kind="Internal").ap()
    hbm["rotT"] = nc.dram_tensor("rotT", [2, PAIRS, P, T], F32, kind="Internal").ap()
    hbm["signs"] = nc.dram_tensor("all_signs", [len(MATS), E, D], BF16, kind="Internal").ap()
    hbm["wvo"] = nc.dram_tensor("wvo", [H * P, D], F32, kind="Internal").ap()

    def sb(owner, name, shape, dt=F32):
        return owner.enter_context(nc.sbuf_tensor(name, shape, dt))

    def two(owner, name, shape):
        return [sb(owner, f"{name}_{n}", shape, F32R) for n in ("hi", "lo")]

    with ExitStack() as ctx:
        keep = {"ident": sb(ctx, "ident", [P, P])}
        place = nc.sbuf_base
        keep["y"] = sb(ctx, "y", [P, NT, D])
        qlatT = [nc.alloc_sbuf_tensor_at(f"qlatT_{n}", [P, KQ, T], F32R, offset=place + i * KQ * T * 4)
                 for i, n in enumerate(("hi", "lo"))]
        keep["abs_sums"], keep["ones"] = sb(ctx, "abs_sums", [P, len(MATS), PAIRS]), sb(ctx, "ones", [P, P])
        keep["abs_total"] = sb(ctx, "abs_total", [P, len(MATS)])
        keep["scale"], keep["bound"] = sb(ctx, "scale", [P, len(MATS)]), sb(ctx, "bound", [P, 2, len(MATS)])
        with ExitStack() as c1:
            keep["kv"] = two(c1, "kv", [P, NT, KVR])
            for n in ("rot", "plain"):
                keep[f"{n}_stored"] = [c1.enter_context(nc.semaphore(f"{n}_stored{g}")) for g in range(2)]
            keep["wvo_stored"] = c1.enter_context(nc.semaphore("wvo_stored"))
            with ExitStack() as c2:
                xT, kvT = two(c2, "xT", [P, KD, T]), two(c2, "kvT", [P, T])
                pair_w = {"raw": sb(c2, "pair_raw", [P, NSL, P]),
                          "split": [two(c2, f"pair{j}", [P, NSL, P]) for j in range(2)]}
                latents(nc, hbm, keep, pair_w, xT, qlatT, kvT)
                heads_inputs(nc, hbm, keep, pair_w, xT, qlatT, kvT)
            attention(nc, hbm, keep)
        ffn = {"wT": [sb(ctx, f"wT_{n}", shape, F32R) for n, shape in
                      (("up", [P, KD, E]), ("gate", [P, KD, E]), ("down", [P, ET, D]))],
               "mv": sb(ctx, "mv3", [P, NT, 2]), "rstd": sb(ctx, "rstd3", [P, NT])}
        turn_signs(nc, hbm, keep, ffn)
        feed_forward(nc, hbm, keep, ffn, out)


def constants():
    freq = (np.float32(1.0) / np.power(np.float32(ROPE_BASE), np.arange(HALF, dtype=np.float32) / np.float32(HALF)))
    angle = (np.arange(T, dtype=np.float32)[:, None] * freq.astype(np.float32)).T
    cos = np.tile(np.cos(angle).astype(np.float32), (4, 1))
    sin = np.tile(np.sin(angle).astype(np.float32), (4, 1))
    sin[P // 2:] *= np.float32(-1.0)
    query, key = np.arange(P)[:, None], np.arange(P)[None, :]
    mask = np.where(key > query, np.float32(NEG), np.float32(0.0)).astype(np.float32)
    return {"ident": np.eye(P, dtype=np.float32), "mask": mask, "cos": cos, "sin": sin}


NAMES = ("x", "Wq_down", "Wq_up", "Wq_rope", "Wkv_down", "Wk_up", "Wk_rope", "Wv_up", "Wo", "W_up", "W_gate", "W_down")


def kernel(**inputs):
    import concourse.bacc as bacc
    from concourse.bass_utils import run_bass_kernel_spmd

    nc = bacc.Bacc("TRN2", target_bir_lowering=False, num_devices=1)
    arrays = {}
    for name in NAMES:
        a = np.ascontiguousarray(inputs[f"L0_{'ffn' if name in ('W_up', 'W_gate', 'W_down') else 'attn'}_{name}"])
        arrays[name] = a.reshape(T, D) if name == "x" else a
    arrays.update(constants())
    hbm = {n: nc.dram_tensor(f"in_{n}", a.shape, mybir.dt.from_np(a.dtype), kind="ExternalInput").ap()
           for n, a in arrays.items()}
    out = nc.dram_tensor("out", [T, D], F32, kind="ExternalOutput").ap()
    program(nc, hbm, out)
    r = run_bass_kernel_spmd(nc, [{f"in_{n}": a for n, a in arrays.items()}], core_ids=[0])
    return r.results[0]["out"].reshape(1, T, D)
```
